# Optimizing a Trainium2 kernel written in Bass

```python
import numpy as np
import jax
import jax.numpy as jnp

def _softmax(x, axis=-1):
    return jax.nn.softmax(x, axis=axis)

def _gelu(x):
    return jax.nn.gelu(x, approximate=True)

def _silu(x):
    return jax.nn.silu(x)

def _sigmoid(x):
    return jax.nn.sigmoid(x)

def _layernorm(x, axis=-1, eps=1e-05):
    m = jnp.mean(x, axis=axis, keepdims=True)
    v = jnp.var(x, axis=axis, keepdims=True)
    return (x - m) / jnp.sqrt(v + eps)

def _scatter_add(tgt, idx, src, axis=0):
    return tgt.at[idx].add(src)

def _segment_sum(src, seg, n):
    return jax.ops.segment_sum(src, seg, n)
kernel_name = 'mk_xattn_seq_d1_seqx_r4_bc1146'

def setup_inputs(seed: int=0):
    np.random.seed(seed)
    _w = jnp.asarray

    def _rec_inputs():
        import jax
        import jax.numpy as jnp
        _rk = jax.random.key(seed)
        x = -0.0003929 + 0.9999 * jax.random.normal(jax.random.fold_in(_rk, 1), (32, 112, 512), jnp.float32)
        _lenS = 112 - jax.random.randint(jax.random.fold_in(_rk, 7), (32,), 0, max(1, 112 // 4) + 1, jnp.int32)
        _lenS2 = 375 - jax.random.randint(jax.random.fold_in(_rk, 8), (32,), 0, max(1, 375 // 4) + 1, jnp.int32)
        _ctx_2048P = jax.random.normal(jax.random.fold_in(_rk, 11), (32, 16, 512), jnp.float32)
        _ctx_2048c = jax.random.dirichlet(jax.random.fold_in(_rk, 511), 0.3 * jnp.ones((16,), jnp.float32), (32, 375))
        _ctx_2048t = jnp.einsum('bsk,bkd->bsd', _ctx_2048c, _ctx_2048P)
        _ctx_2048t = _ctx_2048t * jax.lax.rsqrt(jnp.mean(jnp.square(_ctx_2048t)) + 1e-12) * 0.953939
        ctx_2048 = -8.57375e-05 + 0.999917 * (_ctx_2048t + 0.3 * jax.random.normal(jax.random.fold_in(_rk, 611), (32, 375, 512), jnp.float32))
        _validS = jnp.arange(112)[None, :] < _lenS[:, None]
        _validS2 = jnp.arange(375)[None, :] < _lenS2[:, None]
        _causal = jnp.tril(jnp.ones((112, 112), dtype=bool))
        mask_BxS2_bf1 = jnp.ones((32, 375), dtype=bool)
        return (x, ctx_2048, mask_BxS2_bf1)
    x, ctx_2048, mask_BxS2_bf1 = _rec_inputs()

    def _L0_xattn_setup():
        import jax, jax.numpy as jnp
        import numpy as np
        HIDDEN = 512
        HEADS = 16
        HEAD_DIM = HIDDEN // HEADS
        LN_EPS = 1e-05
        GATE_INIT = 0.5

        def _layer_norm(x, gamma, beta):
            mu = jnp.mean(x, axis=-1, keepdims=True)
            var = jnp.mean(jnp.square(x - mu), axis=-1, keepdims=True)
            return (x - mu) * jax.lax.rsqrt(var + LN_EPS) * gamma + beta
        key = jax.random.key(seed)
        ks = jax.random.split(key, 8)
        B, T_TEXT, T_AUDIO = (4, 512, 375)
        s = 0.02
        return {'hidden_states': jax.random.normal(ks[0], (B, T_TEXT, HIDDEN), jnp.float32), 'audio_kv': jax.random.normal(ks[1], (B, T_AUDIO, HIDDEN), jnp.float32), 'audio_attention_mask': jnp.ones((B, T_AUDIO), dtype=bool), 'Wq': jax.random.normal(ks[2], (HIDDEN, HIDDEN), jnp.float32) * s, 'Wk': jax.random.normal(ks[3], (HIDDEN, HIDDEN), jnp.float32) * s, 'Wv': jax.random.normal(ks[4], (HIDDEN, HIDDEN), jnp.float32) * s, 'Wo': jax.random.normal(ks[5], (HIDDEN, HIDDEN), jnp.float32) * s, 'ln_gamma': jnp.ones((HIDDEN,), jnp.float32), 'ln_beta': jnp.zeros((HIDDEN,), jnp.float32), 'gate': jnp.array([GATE_INIT], jnp.float32)}
    _L0_xattn_all = _L0_xattn_setup()
    _L0_xattn_in = {k: v for k, v in _L0_xattn_all.items() if k in ('Wq', 'Wk', 'Wv', 'Wo', 'ln_gamma', 'ln_beta', 'gate')}
    del _L0_xattn_all
    return {'x': x, 'ctx_2048': ctx_2048, 'mask_BxS2_bf1': mask_BxS2_bf1, 'L0_xattn_Wq': _L0_xattn_in['Wq'], 'L0_xattn_Wk': _L0_xattn_in['Wk'], 'L0_xattn_Wv': _L0_xattn_in['Wv'], 'L0_xattn_Wo': _L0_xattn_in['Wo'], 'L0_xattn_ln_gamma': _L0_xattn_in['ln_gamma'], 'L0_xattn_ln_beta': _L0_xattn_in['ln_beta'], 'L0_xattn_gate': _L0_xattn_in['gate']}

def reference(x, ctx_2048, mask_BxS2_bf1, L0_xattn_Wq, L0_xattn_Wk, L0_xattn_Wv, L0_xattn_Wo, L0_xattn_ln_gamma, L0_xattn_ln_beta, L0_xattn_gate):
    import jax
    import jax.numpy as jnp

    def _L0_xattn_ref(hidden_states, audio_kv, audio_attention_mask, Wq, Wk, Wv, Wo, ln_gamma, ln_beta, gate):
        import jax, jax.numpy as jnp
        import numpy as np
        HIDDEN = 512
        HEADS = 16
        HEAD_DIM = HIDDEN // HEADS
        LN_EPS = 1e-05
        GATE_INIT = 0.5

        def _layer_norm(x, gamma, beta):
            mu = jnp.mean(x, axis=-1, keepdims=True)
            var = jnp.mean(jnp.square(x - mu), axis=-1, keepdims=True)
            return (x - mu) * jax.lax.rsqrt(var + LN_EPS) * gamma + beta
        B, Tt, D = hidden_states.shape
        Ta = audio_kv.shape[1]
        scale = HEAD_DIM ** (-0.5)
        a = _layer_norm(audio_kv, ln_gamma, ln_beta)
        Q = (hidden_states @ Wq.T).reshape(B, Tt, HEADS, HEAD_DIM).transpose(0, 2, 1, 3)
        K = (a @ Wk.T).reshape(B, Ta, HEADS, HEAD_DIM).transpose(0, 2, 1, 3)
        V = (a @ Wv.T).reshape(B, Ta, HEADS, HEAD_DIM).transpose(0, 2, 1, 3)
        scores = jnp.einsum('bhtd,bhsd->bhts', Q, K) * scale
        mask = audio_attention_mask[:, None, None, :]
        scores = jnp.where(mask, scores, jnp.float32(-jnp.inf))
        attn = jax.nn.softmax(scores, axis=-1)
        out = jnp.einsum('bhts,bhsd->bhtd', attn, V)
        out = out.transpose(0, 2, 1, 3).reshape(B, Tt, D)
        out = out @ Wo.T
        return hidden_states + jnp.tanh(gate) * out
    x = _L0_xattn_ref(x, ctx_2048, mask_BxS2_bf1, L0_xattn_Wq, L0_xattn_Wk, L0_xattn_Wv, L0_xattn_Wo, L0_xattn_ln_gamma, L0_xattn_ln_beta, L0_xattn_gate)
    return x

_drawn_inputs = setup_inputs


def setup_inputs(seed=0):
    import zlib

    import numpy as np

    out = dict(_drawn_inputs(seed))
    spreads = {'L0_xattn_ln_gamma': (1.0, 0.6), 'L0_xattn_ln_beta': (0.0, 0.8)}
    factors = {'L0_xattn_Wq': 8.0, 'L0_xattn_Wk': 8.0}
    for name, (base, spread) in spreads.items():
        noise = np.random.default_rng([zlib.crc32(name.encode()), seed]).standard_normal(out[name].shape)
        drawn = base * np.exp(spread * noise) if base else spread * noise
        out[name] = jnp.asarray(drawn.astype(out[name].dtype))
    for name, factor in factors.items():
        out[name] = (out[name] * factor).astype(out[name].dtype)
    return out
```

```python
from contextlib import ExitStack

import concourse.bass as bass
from concourse import mybir

F32 = mybir.dt.float32
F32R = mybir.dt.float32r
U8 = mybir.dt.uint8
ALU = mybir.AluOpType
ACT = mybir.ActivationFunctionType

B, T, S, D = 32, 112, 375, 512
HEADS, HD = 16, 32
KT = D // 128
HC = 128 // HD
ST, SP_ = 3, 125
SE = S + 1
GB = 4
GROUPS = B // GB
GN = GB * T
SLOTS = B * KT
LOOP = 2 * KT
SCALE = float(HD) ** -0.5
EPS = 1e-5
LOWEST = -3.4e38
PASSES = ((0, 0), (0, 1), (1, 0))


def xattn(nc, xT, x, ctx, mask, wqT, wkT, wvT, woT, gamma, beta, gate, out):
    es = ExitStack()
    with es:
        def sb(name, shape, dt=F32):
            return es.enter_context(nc.sbuf_tensor(name, shape, dt))

        def sem(name):
            return es.enter_context(nc.semaphore(name))

        w_kvo = [sb(f"w_{w}", [128, 2, KT, D], F32R) for w in "kvo"]
        wk, wv, wo = w_kvo
        qT = sb("qT", [128, B, KT, T])
        flat = qT[:, :, :, :].rearrange("p b c t -> p (b c t)")
        WN = KT * D
        raw0 = B * KT * T - 4 * WN
        raw_k, raw_v, raw_o, raw_q = [
            flat[:, raw0 + i * WN:raw0 + (i + 1) * WN].rearrange("p (c n) -> p c n", c=KT)
            for i in (1, 2, 3, 0)]
        RAW_GROUP = raw0 // (KT * GN)

        shared_r = sb("shared_r", [128, 2 * WN + 4 * KT * GN], F32R)

        def cut_r(at, *shape):
            n = 1
            for k in shape:
                n *= k
            names = "abcd"[:len(shape)]
            ap = shared_r[:, at:at + n].rearrange(
                f"p ({' '.join(names)}) -> p {' '.join(names)}", **dict(zip(names, shape)))
            return at + n, ap

        at, wq = cut_r(0, 2, KT, D)
        at, xr = cut_r(at, 2, 2, KT, GN)
        at, cT = cut_r(0, 2, 2, KT, SE)
        at, kT = cut_r(at, 2, 2, SE)
        at, qr = cut_r(at, 2, 2, KT, T)
        at, oT = cut_r(at, 2, 2, KT, T)

        shared_f = sb("shared_f", [128, 2 * ST * D + 2 * HC * S + HC * ST * T])
        xraw = shared_f[:, 0:2 * KT * GN].rearrange("p (g c n) -> p g c n", g=2, c=KT)
        v_sb = shared_f[:, 0:2 * ST * D].rearrange("p (b j n) -> p b j n", b=2, j=ST)
        at = 2 * ST * D
        prob = shared_f[:, at:at + 2 * HC * S].rearrange("p (q h s) -> p q h s", q=2, h=HC)
        at += 2 * HC * S
        probT = shared_f[:, at:at + HC * ST * T].rearrange("p (i t) -> p i t", t=T)

        cn = sb("cn", [128, 2, ST, D])
        xy = sb("xy", [128, 2, D])
        mask_u8 = sb("mask_u8", [128, 2, S], U8)
        mask_b = sb("mask_b", [128, 2, S])
        ident = sb("ident", [128, 128])
        gam = sb("gam", [128, KT])
        bet = sb("bet", [128, KT])
        gat = sb("gat", [128, 1])
        bias_kv = sb("bias_kv", [128, 2, KT])
        stats = sb("stats", [128, ST, 6])
        mv = sb("mv", [128, 2, ST, 2])
        half = sb("half", [128, ST])
        vare = sb("vare", [128, ST])
        rs0 = sb("rs0", [128, ST])
        tmp = sb("tmp", [128, ST])
        rstd = sb("rstd", [128, ST])
        nmean = sb("nmean", [128, ST])
        top = sb("top", [128, 2, HC])
        ntop = sb("ntop", [128, 2, HC])
        den = sb("den", [128, 2, HC])
        rden = sb("rden", [128, 2, HC])

        bank = [es.enter_context(nc.psum_tensor(f"bank{i}", [128, 512], F32)) for i in range(8)]
        KPV, VO, PA, PX = 4, 5, 6, 7

        ld_const = sem("ld_const")
        ld_w = {w: sem(f"ld_w{w}") for w in "qkvo"}
        ld_xT = [sem(f"ld_xT{i}") for i in range(2)]
        ld_ctx = [sem(f"ld_ctx{i}") for i in range(2)]
        ld_x = [sem(f"ld_x{i}") for i in range(2)]
        ld_mask = [sem(f"ld_mask{i}") for i in range(2)]
        stored = [sem(f"stored{i}") for i in range(2)]
        ident_done = sem("ident_done")
        ident_step = sem("ident_step")
        pad_done = sem("pad_done")
        wq_hi = sem("wq_hi")
        wq_done = sem("wq_done")
        xr_hi = sem("xr_hi")
        xr_done = sem("xr_done")
        w_hi = sem("w_hi")
        w_done = sem("w_done")
        q_mm = sem("q_mm")
        q_out = sem("q_out")
        bias_mm = sem("bias_mm")
        bias_done = sem("bias_done")
        gate_done = sem("gate_done")
        bn_step = sem("bn_step")
        stats_done = sem("stats_done")
        ln_step = sem("ln_step")
        ln_done = sem("ln_done")
        qr_step = sem("qr_step")
        qr_done = sem("qr_done")
        mask_step = sem("mask_step")
        mask_done = sem("mask_done")
        c_mm = sem("c_mm")
        c_hi = sem("c_hi")
        c_done = sem("c_done")
        k_mm = sem("k_mm")
        k_hi = sem("k_hi")
        k_done = sem("k_done")
        v_mm = sem("v_mm")
        v_done = sem("v_done")
        s_mm = sem("s_mm")
        max_step = sem("max_step")
        max_done = sem("max_done")
        exp_done = sem("exp_done")
        rden_done = sem("rden_done")
        prob_done = sem("prob_done")
        t_mm = [sem(f"t_mm{i}") for i in range(3)]
        t_done = [sem(f"t_done{i}") for i in range(3)]
        pv_mm = sem("pv_mm")
        o_hi = sem("o_hi")
        o_done = sem("o_done")
        y_mm = sem("y_mm")
        y_done = sem("y_done")
        passed = sem("passed")

        block = es.enter_context(nc.Block())

        xT_v = xT.rearrange("(c p) n -> p c n", p=128)
        ctx_v = ctx.rearrange("b (j p) d -> b p j d", p=SP_)
        wT = {"q": wqT, "k": wkT, "v": wvT, "o": woT}

        def live(i, k, shift, count):
            return not isinstance(i, int) or 0 <= k * i + shift < count

        def wait_apart(engine, s, value):
            engine.wait_ge(s, value)
            if not isinstance(value, int):
                engine.sem_inc(passed)

        def slots(engine, slot, first=-1, last=SLOTS // LOOP + 1):
            for i in range(first, 1):
                for r in range(LOOP):
                    slot(i, r)
            with engine.Fori(1, SLOTS // LOOP - 1) as i:
                for r in range(LOOP):
                    slot(i, r)
            for i in range(SLOTS // LOOP - 1, last):
                for r in range(LOOP):
                    slot(i, r)

        def v_item(r):
            b, u = r // KT, r % KT
            return {2: (b + 1, 0), 3: (b + 1, 1), 0: (b, 2), 1: (b, None)}[u]

        @block.sync
        def _(sync):
            def load_xT(i, g):
                sync.dma_start(xraw[:, g, :, :], xT_v[:, :, bass.ds(i * (2 * GN) + g * GN, GN)]) \
                    .then_inc(ld_xT[g], 16)

            def load_w(w, dst):
                sync.dma_start(dst, wT[w].rearrange("(c p) n -> p c n", p=128)).then_inc(ld_w[w], 16)

            def load_ctx(i, c):
                sync.dma_start(cn[0:SP_, c % 2, :, :], ctx_v[i * 2 + c, :, :, :]) \
                    .then_inc(ld_ctx[c % 2], 16)

            def load_mask(i, c):
                sync.dma_start(mask_u8[0:T, c % 2, :],
                               mask[bass.ds(i * 2 + c, 1), :].partition_broadcast(T)
                               .rearrange("p a s -> p (a s)")) \
                    .then_inc(ld_mask[c % 2], 16)

            def load_x(i, c):
                sync.dma_start(xy[0:T, c % 2, :], x[i * 2 + c, :, :]).then_inc(ld_x[c % 2], 16)

            load_w("q", raw_q)
            load_xT(0, 0)
            sync.dma_start(gam[:, :], gamma).then_inc(ld_const, 16)
            sync.dma_start(bet[:, :], beta).then_inc(ld_const, 16)
            sync.dma_start(gat[:, :], gate.partition_broadcast(128)).then_inc(ld_const, 16)
            load_xT(0, 1)
            load_w("k", raw_k)
            load_w("v", raw_v)
            load_w("o", raw_o)
            for b in (0, 1):
                load_ctx(0, b)
                load_mask(0, b)
                load_x(0, b)
            with sync.Fori(1, GROUPS // 2) as i:
                for g in range(2):
                    wait_apart(sync, xr_done, i * 2 + (g - 1))
                    load_xT(i, g)

            def slot(i, r):
                if r % KT:
                    return
                c = r // KT
                if live(i, 2, c + 2, B) and not (isinstance(i, int) and 2 * i + c + 2 < 2):
                    wait_apart(sync, c_mm, i * LOOP + (r + KT))
                    load_ctx(i, c + 2)
                if live(i, 2, c - 1, B):
                    wait_apart(sync, y_done, i * 2 + c)
                    sync.dma_start(out[i * 2 + (c - 1), :, :], xy[0:T, (c + 1) % 2, :]) \
                        .then_inc(stored[(c + 1) % 2], 16)
                    if live(i, 2, c + 1, B):
                        wait_apart(sync, stored[(c + 1) % 2], (i + c) * 16)
                        load_x(i, c + 1)
                if live(i, 2, c + 2, B) and not (isinstance(i, int) and 2 * i + c + 2 < 2):
                    wait_apart(sync, mask_done, i * 2 + (c + 1))
                    load_mask(i, c + 2)

            slots(sync, slot)
            sync.wait_ge(stored[0], 16 * (B // 2))
            sync.wait_ge(stored[1], 16 * (B // 2))

        @block.gpsimd
        def _(pool):
            pool.memset(ident[:, :], 0.0).then_inc(ident_step, 1)
            pool.memset(half[:, :], -0.5).then_inc(ident_step, 1)
            pool.wait_ge(ident_step, 2)
            pool.affine_select(out=ident[:, :], in_=ident[:, :], compare_op=ALU.not_equal, fill=1.0,
                               base=0, pattern=[[-1, 128]], channel_multiplier=1) \
                .then_inc(ident_done, 1)

            def split_q(i, c):
                src = qT[:, bass.ds(i * 2 + c, 1), :, :].rearrange("p a c t -> p (a c) t")
                if not (isinstance(i, int) and 2 * i + c < 2):
                    wait_apart(pool, s_mm, i * LOOP + (c - 1) * KT)
                pool.tensor_copy(qr[:, c % 2, 0, :, :], src).then_inc(qr_step, 1)
                wait_apart(pool, qr_step, i * 2 + (c + 1))
                pool.tensor_tensor(qr[:, c % 2, 1, :, :], src, qr[:, c % 2, 0, :, :].bitcast(F32),
                                   ALU.subtract).then_inc(qr_done, 1)

            def convert_mask(i, c):
                m = mask_b[0:T, c % 2, :]
                wait_apart(pool, ld_mask[c % 2], (i + c // 2 + 1) * 16)
                if not (isinstance(i, int) and 2 * i + c < 2):
                    wait_apart(pool, max_done, i * LOOP + (c - 1) * KT)
                pool.tensor_scalar(m, mask_u8[0:T, c % 2, :], -1.0, 3e38, ALU.add, ALU.mult) \
                    .then_inc(mask_step, 1)
                wait_apart(pool, mask_step, i * 2 + (c + 1))
                pool.tensor_scalar(m, m, 3e38, None, ALU.mult).then_inc(mask_done, 1)

            def normalise(i, c):
                STEPS = 8
                done = [i * (2 * STEPS) + c * STEPS]

                def then(ins):
                    ins.then_inc(ln_step, 1)
                    done[0] = done[0] + 1
                    wait_apart(pool, ln_step, done[0])

                P = SP_
                wait_apart(pool, stats_done, i * 2 + (c + 1))
                then(pool.tensor_scalar(nmean[:P, :], mv[:P, c % 2, :, 0], -1.0, None, ALU.mult))
                then(pool.tensor_scalar(vare[:P, :], mv[:P, c % 2, :, 1], EPS, None, ALU.add))
                then(pool.tensor_tensor(rs0[:P, :], vare[:P, :], half[:P, :], ALU.pow))
                then(pool.tensor_tensor(tmp[:P, :], vare[:P, :], rs0[:P, :], ALU.mult))
                then(pool.tensor_tensor(tmp[:P, :], tmp[:P, :], rs0[:P, :], ALU.mult))
                then(pool.tensor_scalar(tmp[:P, :], tmp[:P, :], -0.5, 1.5, ALU.mult, ALU.add))
                then(pool.tensor_tensor(rstd[:P, :], tmp[:P, :], rs0[:P, :], ALU.mult))
                for j in range(ST):
                    last = pool.tensor_scalar(cn[:P, c % 2, j, :], cn[:P, c % 2, j, :],
                                              nmean[:P, j:j + 1], rstd[:P, j:j + 1],
                                              ALU.add, ALU.mult)
                last.then_inc(ln_step, 1)
                done[0] = done[0] + 1
                wait_apart(pool, ln_step, done[0])
                pool.sem_inc(ln_done, 1)

            def slot(i, r):
                if r % KT:
                    return
                c = r // KT
                if live(i, 2, c + 1, B):
                    split_q(i, c + 1)
                    convert_mask(i, c + 1)
                if live(i, 2, c + 2, B):
                    normalise(i, c + 2)

            pool.wait_ge(q_out, GROUPS)
            pool.memset(cT[:, :, :, :, S:SE].rearrange("p a b c s -> p (a b c) s").bitcast(F32), 0.0) \
                .then_inc(pad_done, 1)
            slots(pool, slot)

        @block.scalar
        def _(act):
            act.wait_ge(ld_const, 48)
            act.activation(gat[:, :], gat[:, :], ACT.Tanh).then_inc(gate_done, 1)
            for w, raw, dst in (("k", raw_k, wk), ("v", raw_v, wv), ("o", raw_o, wo)):
                act.wait_ge(ld_w[w], 16)
                for k in range(KT):
                    scale = 1.0 if w == "o" else gam[:, k:k + 1]
                    act.activation(dst[:, 0, k, :], raw[:, k, :], ACT.Copy, scale=scale) \
                        .then_inc(w_hi, 1)

            def q_group(i, g):
                for m in range(KT):
                    act.wait_ge(q_mm, i * (2 * KT) + (g * KT + m + 1))
                    dst = qT[:, bass.ds(i * (2 * GB) + g * GB, GB), m, :]
                    last = act.activation(dst, bank[KT * g + m][:, 0:GN]
                                          .rearrange("p (b t) -> p b t", t=T), ACT.Copy)
                last.then_inc(q_out, 1)

            q_group(0, 0)
            q_group(0, 1)
            act.wait_ge(bias_mm, 1)
            act.activation(bias_kv[:, :, :].rearrange("p w m -> p (w m)"), bank[0][:, 0:2 * KT],
                           ACT.Copy).then_inc(bias_done, 1)
            act.wait_ge(wq_done, KT)
            act.wait_ge(w_done, 3 * KT)
            with act.Fori(1, GROUPS // 2) as i:
                for g in range(2):
                    q_group(i, g)

            def slot(i, r):
                if live(i, LOOP, r - 2, SLOTS):
                    p, u = (r - 2) // KT % 2, (r - 2) % KT
                    act.wait_ge(pv_mm, i * LOOP + (r - 1))
                    act.activation(oT[:, p, 0, u, :], bank[KPV][:, 0:T], ACT.Identity,
                                   bias=bias_kv[:, 1, u:u + 1]).then_inc(o_hi, 1)
                if live(i, LOOP, r + 5, SLOTS):
                    p, k = (r + 5) // KT % 2, (r + 5) % KT
                    act.wait_ge(c_mm, i * LOOP + (r + 6))
                    act.activation(cT[:, p, 0, k, 0:S], bank[PX][:, 0:S], ACT.Copy).then_inc(c_hi, 1)
                transposed(i, r, 0)
                if live(i, LOOP, r, SLOTS):
                    act.wait_ge(max_done, i * LOOP + (r + 1))
                    for h in range(HC):
                        last = act.activation(prob[0:T, r % 2, h, :], prob[0:T, r % 2, h, :], ACT.Exp,
                                              bias=ntop[0:T, r % 2, h:h + 1], scale=SCALE,
                                              accum_out=den[0:T, r % 2, h:h + 1])
                    last.then_inc(exp_done, 1)
                if live(i, LOOP, r + 1, SLOTS):
                    q, u = (r + 1) % 2, (r + 1) % KT
                    act.wait_ge(k_mm, i * LOOP + (r + 2))
                    act.activation(kT[:, q, 0, :], bank[KPV][:, 0:SE], ACT.Identity,
                                   bias=bias_kv[:, 0, u:u + 1]).then_inc(k_hi, 1)
                transposed(i, r, 2)
                c, j = v_item(r)
                if j is not None and live(i, 2, c, B):
                    act.wait_ge(v_mm, i * (2 * ST) + (c * ST + j + 1))
                    act.activation(v_sb[0:SP_, c % 2, j, :], bank[VO][0:SP_, :], ACT.Copy) \
                        .then_inc(v_done, 1)

            def transposed(i, r, g):
                if live(i, LOOP, r - 1, SLOTS):
                    act.wait_ge(t_mm[g], i * LOOP + r)
                    if not isinstance(i, int) or LOOP * i + r - 1 > 0:
                        act.wait_ge(pv_mm, i * LOOP + (r - 1))
                    act.activation(probT[0:SP_, HC * g:HC * g + HC, :].rearrange("p i t -> p (i t)"),
                                   bank[PA][0:SP_, 0:HC * T], ACT.Copy).then_inc(t_done[g], 1)

            slots(act, slot)

        @block.vector
        def _(dve):
            def split(src, hi, lo, s_hi, count, s_done):
                dve.tensor_copy(hi, src).then_inc(s_hi, 1)
                dve.wait_ge(s_hi, count)
                dve.tensor_tensor(lo, src, hi.bitcast(F32), ALU.subtract).then_inc(s_done, 1)

            dve.wait_ge(ld_w["q"], 16)
            for k in range(KT):
                split(raw_q[:, k, :], wq[:, 0, k, :], wq[:, 1, k, :], wq_hi, k + 1, wq_done)

            def x_group(i, g):
                dve.wait_ge(ld_xT[g], (i + 1) * 16)
                if not isinstance(i, int) or i > 0:
                    dve.wait_ge(q_mm, i * (2 * KT) + (g - 1) * KT)
                split(xraw[:, g, :, :], xr[:, g, 0, :, :], xr[:, g, 1, :, :],
                      xr_hi, i * 2 + (g + 1), xr_done)

            x_group(0, 0)
            x_group(0, 1)
            for n, (w, raw, dst) in enumerate((("k", raw_k, wk), ("v", raw_v, wv), ("o", raw_o, wo))):
                for k in range(KT):
                    dve.wait_ge(w_hi, n * KT + k + 1)
                    scale = 1.0 if w == "o" else gam[:, k:k + 1]
                    dve.scalar_tensor_tensor(dst[:, 1, k, :], raw[:, k, :], scale,
                                             dst[:, 0, k, :].bitcast(F32), ALU.mult, ALU.subtract) \
                        .then_inc(w_done, 1)
            with dve.Fori(1, GROUPS // 2) as i:
                for g in range(2):
                    x_group(i, g)

            def slot(i, r):
                if live(i, LOOP, r - 2, SLOTS):
                    p, u = (r - 2) // KT % 2, (r - 2) % KT
                    dve.wait_ge(o_hi, i * LOOP + (r - 1))
                    dve.scalar_tensor_tensor(oT[:, p, 1, u, :], bank[KPV][:, 0:T],
                                             bias_kv[:, 1, u:u + 1], oT[:, p, 0, u, :].bitcast(F32),
                                             ALU.add, ALU.subtract).then_inc(o_done, 1)
                if live(i, LOOP, r + 5, SLOTS):
                    p, k = (r + 5) // KT % 2, (r + 5) % KT
                    dve.wait_ge(c_hi, i * LOOP + (r + 6))
                    dve.tensor_tensor(cT[:, p, 1, k, 0:S], bank[PX][:, 0:S],
                                      cT[:, p, 0, k, 0:S].bitcast(F32), ALU.subtract) \
                        .then_inc(c_done, 1)
                if live(i, LOOP, r, SLOTS):
                    q, c = r % 2, r // KT
                    if r % KT == 0:
                        dve.wait_ge(mask_done, i * 2 + (c + 1))
                    wait_apart(dve, s_mm, i * LOOP + (r + 1))
                    if not isinstance(i, int) or LOOP * i + r >= 2:
                        wait_apart(dve, t_mm[2], i * LOOP + (r - 1))
                    for h in range(HC):
                        dve.tensor_tensor_reduce(
                            out=prob[0:T, q, h, :], in0=bank[h][0:T, 0:S], in1=mask_b[0:T, c, :],
                            scale=1.0, scalar=LOWEST, op0=ALU.add, op1=ALU.max,
                            accum_out=top[0:T, q, h:h + 1]).then_inc(max_step, 1)
                    dve.wait_ge(max_step, i * (LOOP * HC) + (r + 1) * HC)
                    dve.tensor_scalar(ntop[0:T, q, :], top[0:T, q, :], -SCALE, None, ALU.mult) \
                        .then_inc(max_done, 1)
                if live(i, LOOP, r - 1, SLOTS):
                    dve.wait_ge(t_mm[1], i * LOOP + r)
                    if not isinstance(i, int) or LOOP * i + r - 1 > 0:
                        dve.wait_ge(pv_mm, i * LOOP + (r - 1))
                    dve.tensor_copy(probT[0:SP_, HC:2 * HC, :].rearrange("p i t -> p (i t)"),
                                    bank[PX][0:SP_, 0:HC * T]).then_inc(t_done[1], 1)
                if live(i, LOOP, r + 1, SLOTS):
                    q, u = (r + 1) % 2, (r + 1) % KT
                    dve.wait_ge(k_hi, i * LOOP + (r + 2))
                    dve.scalar_tensor_tensor(kT[:, q, 1, :], bank[KPV][:, 0:SE],
                                             bias_kv[:, 0, u:u + 1], kT[:, q, 0, :].bitcast(F32),
                                             ALU.add, ALU.subtract).then_inc(k_done, 1)
                if live(i, LOOP, r, SLOTS):
                    q = r % 2
                    dve.wait_ge(exp_done, i * LOOP + (r + 1))
                    dve.reciprocal(rden[0:T, q, :], den[0:T, q, :]).then_inc(rden_done, 1)
                    dve.wait_ge(rden_done, i * LOOP + (r + 1))
                    for h in range(HC):
                        last = dve.tensor_scalar(prob[0:T, q, h, :], prob[0:T, q, h, :],
                                                 rden[0:T, q, h:h + 1], None, ALU.mult)
                    last.then_inc(prob_done, 1)
                if r % KT == 0 and live(i, 2, r // KT + 2, B):
                    c = r // KT + 2
                    dve.wait_ge(ld_ctx[c % 2], (i + c // 2 + 1) * 16)
                    if not (isinstance(i, int) and 2 * i + c < 2):
                        dve.wait_ge(ln_done, i * 2 + (c - 1))
                    for j in range(ST):
                        dve.bn_stats(stats[0:SP_, j, :], cn[0:SP_, c % 2, j, :]).then_inc(bn_step, 1)
                    wait_apart(dve, bn_step, i * (2 * ST) + (c + 1) * ST)
                    for j in range(ST):
                        last = dve.bn_aggr(mv[0:SP_, c % 2, j, :], stats[0:SP_, j, :])
                    last.then_inc(stats_done, 1)
                if r % KT == 1 and live(i, 2, r // KT - 1, B):
                    c = r // KT - 1
                    if r == 1:
                        dve.wait_ge(ld_x[1], i * 16)
                    else:
                        dve.wait_ge(ld_x[0], (i + 1) * 16)
                    dve.wait_ge(gate_done, 1)
                    dve.wait_ge(y_mm, i * 2 + (c + 1))
                    dve.scalar_tensor_tensor(xy[0:T, c % 2, :], bank[VO][0:T, :], gat[0:T, 0:1],
                                             xy[0:T, c % 2, :], ALU.mult, ALU.add) \
                        .then_inc(y_done, 1)

            slots(dve, slot)

        @block.tensor
        def _(pe):
            def product(dst, pairs, s_done=None):
                for k, (l, m) in enumerate(pairs):
                    last = pe.matmul(dst, l, m, start=(k == 0), stop=(k == len(pairs) - 1))
                return last

            def q_group(i, g):
                pe.wait_ge(xr_done, i * 2 + (g + 1))
                if not isinstance(i, int) or i > 0:
                    pe.wait_ge(q_out, i * 2 + (g - 1))
                for m in range(KT):
                    product(bank[KT * g + m][:, 0:GN],
                            [(wq[:, a, k, 128 * m:128 * m + 128], xr[:, g, c, k, :])
                             for k in range(KT) for a, c in PASSES]).then_inc(q_mm, 1)

            pe.wait_ge(wq_done, KT)
            q_group(0, 0)
            q_group(0, 1)
            pe.wait_ge(ld_w["k"], 16)
            pe.wait_ge(ld_w["v"], 16)
            pe.wait_ge(ld_const, 48)
            pe.wait_ge(q_out, 1)
            for w, raw in enumerate((raw_k, raw_v)):
                for m in range(KT):
                    last = product(bank[0][:, KT * w + m:KT * w + m + 1],
                                   [(raw[:, k, 128 * m:128 * m + 128], bet[:, k:k + 1])
                                    for k in range(KT)])
            last.then_inc(bias_mm, 1)
            pe.wait_ge(bias_done, 1)
            with pe.Fori(1, GROUPS // 2) as i:
                for g in range(2):
                    q_group(i, g)

            def transpose_probs(i, r, g):
                for e in range(HC):
                    h, j = divmod(HC * g + e, ST)
                    last = pe.transpose(bank[PX if g == 1 else PA][0:SP_, e * T:(e + 1) * T],
                                        prob[0:T, (r - 1) % 2, h, SP_ * j:SP_ * j + SP_],
                                        ident[0:T, 0:T])
                last.then_inc(t_mm[g], 1)

            def slot(i, r):
                here = live(i, LOOP, r, SLOTS)
                before = live(i, LOOP, r - 1, SLOTS)
                if here:
                    c, u, q = r // KT, r % KT, r % 2
                    if u == 0:
                        pe.wait_ge(qr_done, i * 2 + (c + 1))
                    pe.wait_ge(k_done, i * LOOP + (r + 1))
                    if not isinstance(i, int) or LOOP * i + r > 0:
                        pe.wait_ge(max_done, i * LOOP + r)
                    for k, (a, d) in enumerate(PASSES):
                        for h in range(HC):
                            rows = slice(HD * h, HD * h + HD)
                            last = pe.matmul(bank[h][0:T, 0:SE], qr[rows, c, a, u, :], kT[rows, q, d, :],
                                             start=(k == 0), stop=(k == len(PASSES) - 1))
                    last.then_inc(s_mm, 1)
                if before:
                    pe.wait_ge(prob_done, i * LOOP + r)
                    if not isinstance(i, int) or LOOP * i + r - 1 > 0:
                        pe.wait_ge(t_done[2], i * LOOP + (r - 1))
                    transpose_probs(i, r, 0)
                    pe.wait_ge(c_done, i * LOOP + (r + 6) if live(i, LOOP, r + 5, SLOTS) else SLOTS)
                    if not live(i, LOOP, r + 5, SLOTS):
                        pe.wait_ge(t_done[1], i * LOOP + (r - 1))
                    transpose_probs(i, r, 1)
                if live(i, LOOP, r + 1, SLOTS):
                    c, u, q = (r + 1) // KT, (r + 1) % KT, (r + 1) % 2
                    if u == 0:
                        pe.wait_ge(c_done, i * LOOP + (c + 1) * KT)
                        pe.wait_ge(pad_done, 1)
                        pe.wait_ge(w_done, 3 * KT)
                    if live(i, LOOP, r - 2, SLOTS):
                        pe.wait_ge(o_done, i * LOOP + (r - 1))
                    elif not isinstance(i, int) or LOOP * i + r >= 0:
                        pe.wait_ge(k_done, i * LOOP + (r + 1))
                    product(bank[KPV][:, 0:SE],
                            [(wk[:, a, k, 128 * u:128 * u + 128], cT[:, c % 2, d, k, :])
                             for k in range(KT) for a, d in PASSES]).then_inc(k_mm, 1)
                if before:
                    pe.wait_ge(t_done[0], i * LOOP + r)
                    transpose_probs(i, r, 2)
                c, j = v_item(r)
                if j is not None and live(i, 2, c, B):
                    pe.wait_ge(c_done, i * LOOP + (c + 1) * KT)
                    if not (isinstance(i, int) and 2 * i + c == 0 and j == 0):
                        pe.wait_ge(v_done, i * (2 * ST) + (c * ST + j))
                    if j == 0 and (not isinstance(i, int) or 2 * i + c >= 2):
                        pe.wait_ge(y_done, i * 2 + (c - 1))
                    product(bank[VO][0:SP_, :],
                            [(cT[:, c % 2, d, k, SP_ * j:SP_ * j + SP_], wv[:, a, k, :])
                             for k in range(KT) for a, d in PASSES]).then_inc(v_mm, 1)
                if r % KT == 1 and live(i, 2, r // KT - 1, B):
                    c = r // KT - 1
                    pe.wait_ge(o_done, i * LOOP + (c + 1) * KT)
                    if live(i, 2, c + 1, B):
                        pe.wait_ge(v_done, i * (2 * ST) + (c + 2) * ST)
                    else:
                        pe.wait_ge(y_done, i * 2 + c)
                    product(bank[VO][0:T, :],
                            [(oT[:, c % 2, a, k, :], wo[:, d, k, :])
                             for k in range(KT) for a, d in PASSES]).then_inc(y_mm, 1)
                if before:
                    c, u = (r - 1) // KT, (r - 1) % KT
                    for g in range(3):
                        pe.wait_ge(t_done[g], i * LOOP + r)
                    if u == 0:
                        pe.wait_ge(v_done, i * (2 * ST) + (c + 1) * ST)
                    if live(i, LOOP, r + 1, SLOTS):
                        pe.wait_ge(k_done, i * LOOP + (r + 2))
                    else:
                        pe.wait_ge(k_done, SLOTS)
                        pe.wait_ge(o_done, i * LOOP + (r - 1))
                    for j in range(ST):
                        for h in range(HC):
                            col = HD * (HC * u + h)
                            last = pe.matmul(bank[KPV][HD * h:HD * h + HD, 0:T],
                                             v_sb[0:SP_, c % 2, j, col:col + HD],
                                             probT[0:SP_, ST * h + j, :],
                                             start=(j == 0), stop=(j == ST - 1))
                    last.then_inc(pv_mm, 1)
                if live(i, LOOP, r + 6, SLOTS):
                    c, k = (r + 6) // KT, (r + 6) % KT
                    pe.wait_ge(ln_done, i * 2 + (c + 1))
                    if before:
                        pe.wait_ge(t_done[1], i * LOOP + r)
                    elif not isinstance(i, int) or LOOP * i + r + 6 > 0:
                        pe.wait_ge(c_done, i * LOOP + (r + 6))
                    for j in range(ST):
                        last = pe.transpose(bank[PX][:, SP_ * j:SP_ * j + SP_],
                                            cn[0:SP_, c % 2, j, 128 * k:128 * k + 128],
                                            ident[0:SP_, 0:SP_])
                    last.then_inc(c_mm, 1)

            pe.wait_ge(ident_done, 1)
            pe.wait_ge(q_out, GROUPS)
            slots(pe, slot)


def kernel(x, ctx_2048, mask_BxS2_bf1, L0_xattn_Wq, L0_xattn_Wk, L0_xattn_Wv, L0_xattn_Wo,
           L0_xattn_ln_gamma, L0_xattn_ln_beta, L0_xattn_gate):
    import numpy as np
    import concourse.bacc as bacc
    from concourse.bass_utils import run_bass_kernel_spmd

    x = np.ascontiguousarray(x)
    arrays = {
        "in_xT": np.ascontiguousarray(x.reshape(B * T, D).T),
        "in_x": x,
        "in_ctx": np.ascontiguousarray(ctx_2048),
        "in_mask": np.ascontiguousarray(mask_BxS2_bf1).view(np.uint8),
        "in_wqT": np.ascontiguousarray(np.asarray(L0_xattn_Wq).T),
        "in_wkT": np.ascontiguousarray(np.asarray(L0_xattn_Wk).T),
        "in_wvT": np.ascontiguousarray(np.asarray(L0_xattn_Wv).T),
        "in_woT": np.ascontiguousarray(np.asarray(L0_xattn_Wo).T),
        "in_gamma": np.ascontiguousarray(np.asarray(L0_xattn_ln_gamma).reshape(KT, 128).T),
        "in_beta": np.ascontiguousarray(np.asarray(L0_xattn_ln_beta).reshape(KT, 128).T),
        "in_gate": np.ascontiguousarray(L0_xattn_gate),
    }
    nc = bacc.Bacc("TRN2", target_bir_lowering=False, num_devices=1)
    args = [nc.dram_tensor(n, a.shape, mybir.dt.from_np(a.dtype), kind="ExternalInput").ap()
            for n, a in arrays.items()]
    out = nc.dram_tensor("out", (B, T, D), F32, kind="ExternalOutput").ap()
    xattn(nc, *args, out)
    return run_bass_kernel_spmd(nc, [arrays], core_ids=[0]).results[0]["out"]
```

```python
from contextlib import ExitStack

import concourse.bass as bass
from concourse import mybir

F32 = mybir.dt.float32
F32R = mybir.dt.float32r
U8 = mybir.dt.uint8
ALU = mybir.AluOpType
ACT = mybir.ActivationFunctionType

B, T, S, D = 32, 112, 375, 512
HEADS, HD = 16, 32
KT = D // 128
HC = 128 // HD
ST, SP_ = 3, 125
SE = S + 1
GB = 4
GROUPS = B // GB
GN = GB * T
SLOTS = B * KT
LOOP = 2 * KT
SCALE = float(HD) ** -0.5
EPS = 1e-5
HIGHEST = 3.4e38
PASSES = ((0, 0), (0, 1), (1, 0))


def xattn(nc, xT, x, ctx, mask, wqT, wkT, wvT, woT, gamma, beta, gate, out):
    es = ExitStack()
    with es:
        def sb(name, shape, dt=F32):
            return es.enter_context(nc.sbuf_tensor(name, shape, dt))

        def sem(name):
            return es.enter_context(nc.semaphore(name))

        w_kvo = [sb(f"w_{w}", [128, 2, KT, D], F32R) for w in "kvo"]
        wk, wv, wo = w_kvo
        qT = sb("qT", [128, B, KT, T])
        flat = qT[:, :, :, :].rearrange("p b c t -> p (b c t)")
        WN = KT * D
        raw0 = B * KT * T - 4 * WN
        raw_k, raw_v, raw_o, raw_q = [
            flat[:, raw0 + i * WN:raw0 + (i + 1) * WN].rearrange("p (c n) -> p c n", c=KT)
            for i in (1, 2, 3, 0)]
        RAW_GROUP = raw0 // (KT * GN)

        shared_r = sb("shared_r", [128, 2 * WN + 4 * KT * GN], F32R)

        def cut_r(at, *shape):
            n = 1
            for k in shape:
                n *= k
            names = "abcd"[:len(shape)]
            ap = shared_r[:, at:at + n].rearrange(
                f"p ({' '.join(names)}) -> p {' '.join(names)}", **dict(zip(names, shape)))
            return at + n, ap

        at, wq = cut_r(0, 2, KT, D)
        at, xr = cut_r(at, 2, 2, KT, GN)
        at, cT = cut_r(0, 2, 2, KT, SE)
        at, kT = cut_r(at, 2, 2, SE)
        at, qr = cut_r(at, 2, 2, KT, T)
        at, oT = cut_r(at, 2, 2, KT, T)

        shared_f = sb("shared_f", [128, 2 * ST * D + 2 * HC * S + HC * ST * T])
        xraw = shared_f[:, 0:2 * KT * GN].rearrange("p (g c n) -> p g c n", g=2, c=KT)
        v_sb = shared_f[:, 0:2 * ST * D].rearrange("p (b j n) -> p b j n", b=2, j=ST)
        at = 2 * ST * D
        prob = shared_f[:, at:at + 2 * HC * S].rearrange("p (q h s) -> p q h s", q=2, h=HC)
        at += 2 * HC * S
        probT = shared_f[:, at:at + HC * ST * T].rearrange("p (i t) -> p i t", t=T)

        cn = sb("cn", [128, 2, ST, D])
        xy = sb("xy", [128, 2, D])
        mask_u8 = sb("mask_u8", [128, 2, S], U8)
        mask_b = sb("mask_b", [128, 2, S])
        ident = sb("ident", [128, 128])
        gam = sb("gam", [128, KT])
        bet = sb("bet", [128, KT])
        gat = sb("gat", [128, 1])
        bias_kv = sb("bias_kv", [128, 2, KT])
        stats = sb("stats", [128, ST, 6])
        mv = sb("mv", [128, 2, ST, 2])
        half = sb("half", [128, ST])
        vare = sb("vare", [128, ST])
        rs0 = sb("rs0", [128, ST])
        tmp = sb("tmp", [128, ST])
        rstd = sb("rstd", [128, ST])
        nmean = sb("nmean", [128, ST])
        ntop = sb("ntop", [128, 2, HC])
        den = sb("den", [128, 2, HC])
        rden = sb("rden", [128, 2, HC])

        bank = [es.enter_context(nc.psum_tensor(f"bank{i}", [128, 512], F32)) for i in range(8)]
        KB, VO, PA, PX = 4, 5, 6, 7

        ld_const = sem("ld_const")
        ld_w = {w: sem(f"ld_w{w}") for w in "kvo"}
        ld_wq = [sem(f"ld_wq{k}") for k in range(KT)]
        ld_x0 = [sem(f"ld_x0{k}") for k in range(KT)]
        ld_xT = [sem(f"ld_xT{i}") for i in range(2)]
        ld_ctx = [sem(f"ld_ctx{i}") for i in range(2)]
        ld_x = [sem(f"ld_x{i}") for i in range(2)]
        ld_mask = [sem(f"ld_mask{i}") for i in range(2)]
        stored = [sem(f"stored{i}") for i in range(2)]
        ident_done = sem("ident_done")
        ident_step = sem("ident_step")
        pad_done = sem("pad_done")
        wq_hi = sem("wq_hi")
        wq_done = sem("wq_done")
        x0_hi = sem("x0_hi")
        x0_done = sem("x0_done")
        xr_hi = sem("xr_hi")
        xr_done = sem("xr_done")
        w_hi = sem("w_hi")
        w_done = sem("w_done")
        q_mm = sem("q_mm")
        q_out = sem("q_out")
        bias_mm = sem("bias_mm")
        bias_done = sem("bias_done")
        gate_done = sem("gate_done")
        bn_step = sem("bn_step")
        stats_done = sem("stats_done")
        ln_step = sem("ln_step")
        ln_done = sem("ln_done")
        qr_step = sem("qr_step")
        qr_done = sem("qr_done")
        mask_step = sem("mask_step")
        mask_done = sem("mask_done")
        c_mm = sem("c_mm")
        c_hi = sem("c_hi")
        c_done = sem("c_done")
        k_mm = sem("k_mm")
        k_hi = sem("k_hi")
        k_done = sem("k_done")
        v_mm = sem("v_mm")
        v_done = sem("v_done")
        s_mm = sem("s_mm")
        max_done = sem("max_done")
        exp_done = sem("exp_done")
        rden_done = sem("rden_done")
        prob_done = sem("prob_done")
        t_mm = [sem(f"t_mm{i}") for i in range(3)]
        t_done = [sem(f"t_done{i}") for i in range(3)]
        pv_mm = sem("pv_mm")
        o_hi = sem("o_hi")
        o_done = sem("o_done")
        y_mm = sem("y_mm")
        y_done = sem("y_done")
        passed = sem("passed")

        block = es.enter_context(nc.Block())

        xT_v = xT.rearrange("(c p) n -> p c n", p=128)
        ctx_v = ctx.rearrange("b (j p) d -> b p j d", p=SP_)
        wqT_v = wqT.rearrange("(c p) n -> p c n", p=128)
        wT = {"k": wkT, "v": wvT, "o": woT}

        def live(i, k, shift, count):
            return not isinstance(i, int) or 0 <= k * i + shift < count

        def first_two(i, c):
            return isinstance(i, int) and 2 * i + c < 2

        def wait_apart(engine, s, value):
            engine.wait_ge(s, value)
            if not isinstance(value, int):
                engine.sem_inc(passed)

        def c_bank(i, r):
            return PA if isinstance(i, int) and LOOP * i + r < 0 and r % 2 else PX

        def slots(engine, slot, first=-1, last=SLOTS // LOOP + 1):
            for i in range(first, 1):
                for r in range(LOOP):
                    slot(i, r)
            with engine.Fori(1, SLOTS // LOOP - 1) as i:
                for r in range(LOOP):
                    slot(i, r)
            for i in range(SLOTS // LOOP - 1, last):
                for r in range(LOOP):
                    slot(i, r)

        def v_item(r):
            b, u = r // KT, r % KT
            return {2: (b + 1, 0), 3: (b + 1, 1), 0: (b, 2), 1: (b, None)}[u]

        @block.sync
        def _(sync):
            def load_xT(i, g):
                sync.dma_start(xraw[:, g, :, :], xT_v[:, :, bass.ds(i * (2 * GN) + g * GN, GN)]) \
                    .then_inc(ld_xT[g], 16)

            def load_w(w, dst):
                sync.dma_start(dst, wT[w].rearrange("(c p) n -> p c n", p=128)).then_inc(ld_w[w], 16)

            def load_ctx(i, c):
                sync.dma_start(cn[0:SP_, c % 2, :, :], ctx_v[i * 2 + c, :, :, :]) \
                    .then_inc(ld_ctx[c % 2], 16)

            def load_mask(i, c):
                sync.dma_start(mask_u8[0:T, c % 2, :],
                               mask[bass.ds(i * 2 + c, 1), :].partition_broadcast(T)
                               .rearrange("p a s -> p (a s)")) \
                    .then_inc(ld_mask[c % 2], 16)

            def load_x(i, c):
                sync.dma_start(xy[0:T, c % 2, :], x[i * 2 + c, :, :]).then_inc(ld_x[c % 2], 16)

            for k in range(KT):
                sync.dma_start(raw_q[:, k, :], wqT_v[:, k, :]).then_inc(ld_wq[k], 16)
            sync.dma_start(gam[:, :], gamma).then_inc(ld_const, 16)
            sync.dma_start(bet[:, :], beta).then_inc(ld_const, 16)
            sync.dma_start(gat[:, :], gate.partition_broadcast(128)).then_inc(ld_const, 16)
            load_xT(0, 1)
            load_w("k", raw_k)
            load_w("v", raw_v)
            load_w("o", raw_o)
            for b in (0, 1):
                load_ctx(0, b)
                load_mask(0, b)
                load_x(0, b)
            with sync.Fori(1, GROUPS // 2) as i:
                for g in range(2):
                    wait_apart(sync, xr_done, i * 2 + (g - 1))
                    load_xT(i, g)

            def slot(i, r):
                if r % KT:
                    return
                c = r // KT
                if live(i, 2, c + 2, B) and not first_two(i, c + 2):
                    wait_apart(sync, c_mm, i * LOOP + (r + KT))
                    load_ctx(i, c + 2)
                if live(i, 2, c - 1, B):
                    wait_apart(sync, y_done, i * 2 + c)
                    sync.dma_start(out[i * 2 + (c - 1), :, :], xy[0:T, (c + 1) % 2, :]) \
                        .then_inc(stored[(c + 1) % 2], 16)
                    if live(i, 2, c + 1, B):
                        wait_apart(sync, stored[(c + 1) % 2], (i + c) * 16)
                        load_x(i, c + 1)
                if live(i, 2, c + 2, B) and not first_two(i, c + 2):
                    wait_apart(sync, mask_done, i * 2 + (c + 1))
                    load_mask(i, c + 2)

            slots(sync, slot)
            sync.wait_ge(stored[0], 16 * (B // 2))
            sync.wait_ge(stored[1], 16 * (B // 2))

        @block.gpsimd
        def _(pool):
            pool.memset(ident[:, :], 0.0).then_inc(ident_step, 1)
            pool.memset(half[:, :], -0.5).then_inc(ident_step, 1)
            pool.wait_ge(ident_step, 2)
            pool.affine_select(out=ident[:, :], in_=ident[:, :], compare_op=ALU.not_equal, fill=1.0,
                               base=0, pattern=[[-1, 128]], channel_multiplier=1) \
                .then_inc(ident_done, 1)

            def split_q(i, c):
                src = qT[:, bass.ds(i * 2 + c, 1), :, :].rearrange("p a c t -> p (a c) t")
                if not first_two(i, c):
                    wait_apart(pool, s_mm, i * LOOP + (c - 1) * KT)
                pool.tensor_copy(qr[:, c % 2, 0, :, :], src).then_inc(qr_step, 1)
                wait_apart(pool, qr_step, i * 2 + (c + 1))
                pool.tensor_tensor(qr[:, c % 2, 1, :, :], src, qr[:, c % 2, 0, :, :].bitcast(F32),
                                   ALU.subtract).then_inc(qr_done, 1)

            def convert_mask(i, c):
                m = mask_b[0:T, c % 2, :]
                wait_apart(pool, ld_mask[c % 2], (i + c // 2 + 1) * 16)
                if not first_two(i, c):
                    wait_apart(pool, max_done, i * (LOOP * HC) + (c - 1) * KT * HC)
                pool.tensor_scalar(m, mask_u8[0:T, c % 2, :], -1.0, 3e38, ALU.add, ALU.mult) \
                    .then_inc(mask_step, 1)
                wait_apart(pool, mask_step, i * 2 + (c + 1))
                pool.tensor_scalar(m, m, 3e38, None, ALU.mult).then_inc(mask_done, 1)

            def normalise(i, c):
                STEPS = 8
                done = [i * (2 * STEPS) + c * STEPS]

                def then(ins):
                    ins.then_inc(ln_step, 1)
                    done[0] = done[0] + 1
                    wait_apart(pool, ln_step, done[0])

                P = SP_
                wait_apart(pool, stats_done, i * 2 + (c + 1))
                then(pool.tensor_scalar(nmean[:P, :], mv[:P, c % 2, :, 0], -1.0, None, ALU.mult))
                then(pool.tensor_scalar(vare[:P, :], mv[:P, c % 2, :, 1], EPS, None, ALU.add))
                then(pool.tensor_tensor(rs0[:P, :], vare[:P, :], half[:P, :], ALU.pow))
                then(pool.tensor_tensor(tmp[:P, :], vare[:P, :], rs0[:P, :], ALU.mult))
                then(pool.tensor_tensor(tmp[:P, :], tmp[:P, :], rs0[:P, :], ALU.mult))
                then(pool.tensor_scalar(tmp[:P, :], tmp[:P, :], -0.5, 1.5, ALU.mult, ALU.add))
                then(pool.tensor_tensor(rstd[:P, :], tmp[:P, :], rs0[:P, :], ALU.mult))
                for j in range(ST):
                    last = pool.tensor_scalar(cn[:P, c % 2, j, :], cn[:P, c % 2, j, :],
                                              nmean[:P, j:j + 1], rstd[:P, j:j + 1],
                                              ALU.add, ALU.mult)
                last.then_inc(ln_step, 1)
                done[0] = done[0] + 1
                wait_apart(pool, ln_step, done[0])
                pool.sem_inc(ln_done, 1)

            def slot(i, r):
                if r % KT:
                    return
                c = r // KT
                if live(i, 2, c + 1, B):
                    split_q(i, c + 1)
                    convert_mask(i, c + 1)
                if live(i, 2, c + 2, B) and not first_two(i, c + 2):
                    normalise(i, c + 2)

            normalise(-1, 2)
            normalise(-1, 3)
            pool.wait_ge(q_out, GROUPS)
            pool.memset(cT[:, :, :, :, S:SE].rearrange("p a b c s -> p (a b c) s").bitcast(F32), 0.0) \
                .then_inc(pad_done, 1)
            slots(pool, slot)

        @block.scalar
        def _(act):
            for k in range(KT):
                act.dma_start(xraw[:, 0, k, :], xT_v[:, k, 0:GN]).then_inc(ld_x0[k], 16)
            for k in range(KT):
                act.wait_ge(ld_wq[k], 16)
                act.activation(wq[:, 0, k, :], raw_q[:, k, :], ACT.Copy).then_inc(wq_hi, 1)
            act.wait_ge(ld_const, 48)
            act.activation(gat[:, :], gat[:, :], ACT.Tanh).then_inc(gate_done, 1)
            for w, raw, dst in (("k", raw_k, wk), ("v", raw_v, wv), ("o", raw_o, wo)):
                act.wait_ge(ld_w[w], 16)
                for k in range(KT):
                    scale = 1.0 if w == "o" else gam[:, k:k + 1]
                    act.activation(dst[:, 0, k, :], raw[:, k, :], ACT.Copy, scale=scale) \
                        .then_inc(w_hi, 1)

            def q_group(i, g):
                for m in range(KT):
                    act.wait_ge(q_mm, i * (2 * KT) + (g * KT + m + 1))
                    dst = qT[:, bass.ds(i * (2 * GB) + g * GB, GB), m, :]
                    last = act.activation(dst, bank[KT * g + m][:, 0:GN]
                                          .rearrange("p (b t) -> p b t", t=T), ACT.Copy)
                last.then_inc(q_out, 1)

            q_group(0, 0)
            q_group(0, 1)
            act.wait_ge(bias_mm, 1)
            act.activation(bias_kv[:, :, :].rearrange("p w m -> p (w m)"), bank[0][:, 0:2 * KT],
                           ACT.Copy).then_inc(bias_done, 1)
            act.wait_ge(wq_done, KT)
            act.wait_ge(w_done, 3 * KT)
            with act.Fori(1, GROUPS // 2) as i:
                for g in range(2):
                    q_group(i, g)

            def slot(i, r):
                if live(i, LOOP, r - 2, SLOTS):
                    p, u = (r - 2) // KT % 2, (r - 2) % KT
                    act.wait_ge(pv_mm, i * LOOP + (r - 1))
                    act.activation(oT[:, p, 0, u, :], bank[VO][:, 0:T], ACT.Identity,
                                   bias=bias_kv[:, 1, u:u + 1]).then_inc(o_hi, 1)
                transposed(i, r, 0)
                ending = not live(i, LOOP, r + 2, SLOTS)
                if ending:
                    transposed(i, r, 2)
                if live(i, LOOP, r, SLOTS):
                    for h in range(HC):
                        act.wait_ge(max_done, i * (LOOP * HC) + (r * HC + h + 1))
                        last = act.activation(prob[0:T, r % 2, h, :], prob[0:T, r % 2, h, :], ACT.Exp,
                                              bias=ntop[0:T, r % 2, h:h + 1], scale=-1.0,
                                              accum_out=den[0:T, r % 2, h:h + 1])
                    last.then_inc(exp_done, 1)
                c, j = v_item(r)
                if j is not None and live(i, 2, c, B):
                    act.wait_ge(v_mm, i * (2 * ST) + (c * ST + j + 1))
                    act.activation(v_sb[0:SP_, c % 2, j, :], bank[VO][0:SP_, :], ACT.Copy) \
                        .then_inc(v_done, 1)
                if not ending:
                    transposed(i, r, 2)
                if live(i, LOOP, r + 6, SLOTS):
                    p, k = (r + 6) // KT % 2, (r + 6) % KT
                    act.wait_ge(c_mm, i * LOOP + (r + 7))
                    act.activation(cT[:, p, 0, k, 0:S], bank[c_bank(i, r)][:, 0:S], ACT.Copy) \
                        .then_inc(c_hi, 1)
                if live(i, LOOP, r + 2, SLOTS):
                    q, u = (r + 2) % 2, (r + 2) % KT
                    act.wait_ge(k_mm, i * LOOP + (r + 3))
                    act.activation(kT[:, q, 0, :], bank[KB][:, 0:SE], ACT.Identity,
                                   bias=bias_kv[:, 0, u:u + 1]).then_inc(k_hi, 1)

            def transposed(i, r, g):
                if live(i, LOOP, r - 1, SLOTS):
                    act.wait_ge(t_mm[g], i * LOOP + r)
                    if not isinstance(i, int) or LOOP * i + r - 1 > 0:
                        act.wait_ge(pv_mm, i * LOOP + (r - 1))
                    act.activation(probT[0:SP_, HC * g:HC * g + HC, :].rearrange("p i t -> p (i t)"),
                                   bank[PA][0:SP_, 0:HC * T], ACT.Copy).then_inc(t_done[g], 1)

            slots(act, slot)

        @block.vector
        def _(dve):
            def split(src, hi, lo, s_hi, count, s_done):
                dve.tensor_copy(hi, src).then_inc(s_hi, 1)
                dve.wait_ge(s_hi, count)
                dve.tensor_tensor(lo, src, hi.bitcast(F32), ALU.subtract).then_inc(s_done, 1)

            for k in range(KT):
                dve.wait_ge(ld_x0[k], 16)
                dve.tensor_copy(xr[:, 0, 0, k, :], xraw[:, 0, k, :]).then_inc(x0_hi, 1)
                dve.wait_ge(wq_hi, k + 1)
                dve.tensor_tensor(wq[:, 1, k, :], raw_q[:, k, :], wq[:, 0, k, :].bitcast(F32),
                                  ALU.subtract).then_inc(wq_done, 1)
                dve.wait_ge(x0_hi, k + 1)
                dve.tensor_tensor(xr[:, 0, 1, k, :], xraw[:, 0, k, :],
                                  xr[:, 0, 0, k, :].bitcast(F32), ALU.subtract) \
                    .then_inc(x0_done if k < KT - 1 else xr_done, 1)

            def x_group(i, g):
                dve.wait_ge(ld_xT[g], (i + g) * 16)
                if not isinstance(i, int) or i > 0:
                    dve.wait_ge(q_mm, i * (2 * KT) + (g - 1) * KT)
                split(xraw[:, g, :, :], xr[:, g, 0, :, :], xr[:, g, 1, :, :],
                      xr_hi, i * 2 + g, xr_done)

            def statistics(i, c):
                dve.wait_ge(ld_ctx[c % 2], (i + c // 2 + 1) * 16)
                if not first_two(i, c):
                    dve.wait_ge(ln_done, i * 2 + (c - 1))
                elif 2 * i + c == 1:
                    dve.wait_ge(stats_done, 1)
                for j in range(ST):
                    dve.bn_stats(stats[0:SP_, j, :], cn[0:SP_, c % 2, j, :]).then_inc(bn_step, 1)
                wait_apart(dve, bn_step, i * (2 * ST) + (c + 1) * ST)
                for j in range(ST):
                    last = dve.bn_aggr(mv[0:SP_, c % 2, j, :], stats[0:SP_, j, :])
                last.then_inc(stats_done, 1)

            x_group(0, 1)
            for n, (w, raw, dst) in enumerate((("k", raw_k, wk), ("v", raw_v, wv), ("o", raw_o, wo))):
                for k in range(KT):
                    dve.wait_ge(w_hi, n * KT + k + 1)
                    scale = 1.0 if w == "o" else gam[:, k:k + 1]
                    dve.scalar_tensor_tensor(dst[:, 1, k, :], raw[:, k, :], scale,
                                             dst[:, 0, k, :].bitcast(F32), ALU.mult, ALU.subtract) \
                        .then_inc(w_done, 1)
            statistics(-1, 2)
            statistics(-1, 3)
            with dve.Fori(1, GROUPS // 2) as i:
                for g in range(2):
                    x_group(i, g)

            def slot(i, r):
                if live(i, LOOP, r - 2, SLOTS):
                    p, u = (r - 2) // KT % 2, (r - 2) % KT
                    dve.wait_ge(o_hi, i * LOOP + (r - 1))
                    dve.scalar_tensor_tensor(oT[:, p, 1, u, :], bank[VO][:, 0:T],
                                             bias_kv[:, 1, u:u + 1], oT[:, p, 0, u, :].bitcast(F32),
                                             ALU.add, ALU.subtract).then_inc(o_done, 1)
                if live(i, LOOP, r, SLOTS):
                    q, c = r % 2, r // KT
                    if r % KT == 0:
                        dve.wait_ge(mask_done, i * 2 + (c + 1))
                    wait_apart(dve, s_mm, i * LOOP + (r + 1))
                    if not isinstance(i, int) or LOOP * i + r >= 2:
                        wait_apart(dve, t_mm[2], i * LOOP + (r - 1))
                    for h in range(HC):
                        dve.tensor_tensor_reduce(
                            out=prob[0:T, q, h, :], in0=bank[h][0:T, 0:S], in1=mask_b[0:T, c, :],
                            scale=-SCALE, scalar=HIGHEST, op0=ALU.add, op1=ALU.min,
                            accum_out=ntop[0:T, q, h:h + 1]).then_inc(max_done, 1)
                if live(i, LOOP, r - 1, SLOTS):
                    dve.wait_ge(t_mm[1], i * LOOP + r)
                    if not isinstance(i, int) or LOOP * i + r - 1 > 0:
                        dve.wait_ge(pv_mm, i * LOOP + (r - 1))
                    dve.tensor_copy(probT[0:SP_, HC:2 * HC, :].rearrange("p i t -> p (i t)"),
                                    bank[PX][0:SP_, 0:HC * T]).then_inc(t_done[1], 1)
                if r % KT == 0 and live(i, 2, r // KT + 2, B) and not first_two(i, r // KT + 2):
                    statistics(i, r // KT + 2)
                if r % KT == 1 and live(i, 2, r // KT - 1, B):
                    c = r // KT - 1
                    if r == 1:
                        dve.wait_ge(ld_x[1], i * 16)
                    else:
                        dve.wait_ge(ld_x[0], (i + 1) * 16)
                    dve.wait_ge(gate_done, 1)
                    dve.wait_ge(y_mm, i * 2 + (c + 1))
                    dve.scalar_tensor_tensor(xy[0:T, c % 2, :], bank[VO][0:T, :], gat[0:T, 0:1],
                                             xy[0:T, c % 2, :], ALU.mult, ALU.add) \
                        .then_inc(y_done, 1)
                if live(i, LOOP, r, SLOTS):
                    q = r % 2
                    dve.wait_ge(exp_done, i * LOOP + (r + 1))
                    dve.reciprocal(rden[0:T, q, :], den[0:T, q, :]).then_inc(rden_done, 1)
                    dve.wait_ge(rden_done, i * LOOP + (r + 1))
                    for h in range(HC):
                        last = dve.tensor_scalar(prob[0:T, q, h, :], prob[0:T, q, h, :],
                                                 rden[0:T, q, h:h + 1], None, ALU.mult)
                    last.then_inc(prob_done, 1)
                if live(i, LOOP, r + 6, SLOTS):
                    p, k = (r + 6) // KT % 2, (r + 6) % KT
                    dve.wait_ge(c_hi, i * LOOP + (r + 7))
                    dve.tensor_tensor(cT[:, p, 1, k, 0:S], bank[c_bank(i, r)][:, 0:S],
                                      cT[:, p, 0, k, 0:S].bitcast(F32), ALU.subtract) \
                        .then_inc(c_done, 1)
                if live(i, LOOP, r + 2, SLOTS):
                    q, u = (r + 2) % 2, (r + 2) % KT
                    dve.wait_ge(k_hi, i * LOOP + (r + 3))
                    dve.scalar_tensor_tensor(kT[:, q, 1, :], bank[KB][:, 0:SE],
                                             bias_kv[:, 0, u:u + 1], kT[:, q, 0, :].bitcast(F32),
                                             ALU.add, ALU.subtract).then_inc(k_done, 1)

            slots(dve, slot)

        @block.tensor
        def _(pe):
            def product(dst, pairs, s_done=None):
                for k, (l, m) in enumerate(pairs):
                    last = pe.matmul(dst, l, m, start=(k == 0), stop=(k == len(pairs) - 1))
                return last

            def q_group(i, g):
                if not isinstance(i, int) or g > 0:
                    pe.wait_ge(xr_done, i * 2 + (g + 1))
                if not isinstance(i, int) or i > 0:
                    pe.wait_ge(q_out, i * 2 + (g - 1))
                for k in range(KT):
                    if isinstance(i, int) and g == 0:
                        pe.wait_ge(wq_done, k + 1)
                        pe.wait_ge(x0_done, k + 1) if k < KT - 1 else pe.wait_ge(xr_done, 1)
                    for m in range(KT):
                        for e, (a, c) in enumerate(PASSES):
                            last = pe.matmul(bank[KT * g + m][:, 0:GN],
                                             wq[:, a, k, 128 * m:128 * m + 128], xr[:, g, c, k, :],
                                             start=(k == 0 and e == 0),
                                             stop=(k == KT - 1 and e == len(PASSES) - 1))
                        if k == KT - 1:
                            last.then_inc(q_mm, 1)

            q_group(0, 0)
            q_group(0, 1)
            pe.wait_ge(ld_w["k"], 16)
            pe.wait_ge(ld_w["v"], 16)
            pe.wait_ge(ld_const, 48)
            pe.wait_ge(q_out, 1)
            for w, raw in enumerate((raw_k, raw_v)):
                for m in range(KT):
                    last = product(bank[0][:, KT * w + m:KT * w + m + 1],
                                   [(raw[:, k, 128 * m:128 * m + 128], bet[:, k:k + 1])
                                    for k in range(KT)])
            last.then_inc(bias_mm, 1)
            pe.wait_ge(bias_done, 1)
            with pe.Fori(1, GROUPS // 2) as i:
                for g in range(2):
                    q_group(i, g)

            def transpose_probs(i, r, g):
                for e in range(HC):
                    h, j = divmod(HC * g + e, ST)
                    last = pe.transpose(bank[PX if g == 1 else PA][0:SP_, e * T:(e + 1) * T],
                                        prob[0:T, (r - 1) % 2, h, SP_ * j:SP_ * j + SP_],
                                        ident[0:T, 0:T])
                last.then_inc(t_mm[g], 1)

            def slot(i, r):
                here = live(i, LOOP, r, SLOTS)
                before = live(i, LOOP, r - 1, SLOTS)
                if here:
                    c, u, q = r // KT, r % KT, r % 2
                    if u == 0:
                        pe.wait_ge(qr_done, i * 2 + (c + 1))
                    pe.wait_ge(k_done, i * LOOP + (r + 1))
                    if not isinstance(i, int) or LOOP * i + r > 0:
                        pe.wait_ge(max_done, i * (LOOP * HC) + r * HC)
                    for k, (a, d) in enumerate(PASSES):
                        for h in range(HC):
                            rows = slice(HD * h, HD * h + HD)
                            last = pe.matmul(bank[h][0:T, 0:SE], qr[rows, c, a, u, :], kT[rows, q, d, :],
                                             start=(k == 0), stop=(k == len(PASSES) - 1))
                    last.then_inc(s_mm, 1)
                if before:
                    pe.wait_ge(prob_done, i * LOOP + r)
                    if not isinstance(i, int) or LOOP * i + r - 1 > 0:
                        pe.wait_ge(t_done[2], i * LOOP + (r - 1))
                    pe.wait_ge(c_done, i * LOOP + (r + 6) if live(i, LOOP, r + 5, SLOTS) else SLOTS)
                    if not live(i, LOOP, r + 5, SLOTS):
                        pe.wait_ge(t_done[1], i * LOOP + (r - 1))
                    transpose_probs(i, r, 0)
                    transpose_probs(i, r, 1)
                c, j = v_item(r)
                v_live = j is not None and live(i, 2, c, B)
                if v_live:
                    pe.wait_ge(c_done, i * LOOP + (c + 1) * KT)
                    if live(i, LOOP, r - 2, SLOTS):
                        pe.wait_ge(o_done, i * LOOP + (r - 1))
                    elif 2 * i + c > 0 or j > 0:
                        pe.wait_ge(v_done, i * (2 * ST) + (c * ST + j))
                    product(bank[VO][0:SP_, :],
                            [(cT[:, c % 2, d, k, SP_ * j:SP_ * j + SP_], wv[:, a, k, :])
                             for k in range(KT) for a, d in PASSES]).then_inc(v_mm, 1)
                o_live = r % KT == 1 and live(i, 2, r // KT - 1, B)
                if o_live:
                    c = r // KT - 1
                    pe.wait_ge(o_done, i * LOOP + (c + 1) * KT)
                    product(bank[VO][0:T, :],
                            [(oT[:, c % 2, a, k, :], wo[:, d, k, :])
                             for k in range(KT) for a, d in PASSES]).then_inc(y_mm, 1)
                if before:
                    pe.wait_ge(t_done[0], i * LOOP + r)
                    transpose_probs(i, r, 2)
                if live(i, LOOP, r + 6, SLOTS):
                    c, k = (r + 6) // KT, (r + 6) % KT
                    pe.wait_ge(ln_done, i * 2 + (c + 1))
                    if before:
                        pe.wait_ge(t_done[1], i * LOOP + r)
                    elif LOOP * i + r + 6 >= 2:
                        pe.wait_ge(c_done, LOOP * i + r + 5)
                    for j in range(ST):
                        last = pe.transpose(bank[c_bank(i, r)][:, SP_ * j:SP_ * j + SP_],
                                            cn[0:SP_, c % 2, j, 128 * k:128 * k + 128],
                                            ident[0:SP_, 0:SP_])
                    last.then_inc(c_mm, 1)
                if live(i, LOOP, r + 2, SLOTS):
                    c, u = (r + 2) // KT, (r + 2) % KT
                    if u == 0:
                        pe.wait_ge(c_done, i * LOOP + (c + 1) * KT)
                        pe.wait_ge(pad_done, 1)
                        pe.wait_ge(w_done, 3 * KT)
                    if not isinstance(i, int) or LOOP * i + r + 2 > 0:
                        pe.wait_ge(k_done, i * LOOP + (r + 2))
                    product(bank[KB][:, 0:SE],
                            [(wk[:, a, k, 128 * u:128 * u + 128], cT[:, c % 2, d, k, :])
                             for k in range(KT) for a, d in PASSES]).then_inc(k_mm, 1)
                if before:
                    c, u = (r - 1) // KT, (r - 1) % KT
                    for g in range(3):
                        pe.wait_ge(t_done[g], i * LOOP + r)
                    if u == 0:
                        pe.wait_ge(v_done, i * (2 * ST) + (c + 1) * ST)
                    vc, vj = v_item(r)
                    if v_live:
                        pe.wait_ge(v_done, i * (2 * ST) + (vc * ST + vj + 1))
                    elif o_live:
                        pe.wait_ge(y_done, i * 2 + r // KT)
                    elif live(i, LOOP, r - 2, SLOTS):
                        pe.wait_ge(o_done, i * LOOP + (r - 1))
                    for j in range(ST):
                        for h in range(HC):
                            col = HD * (HC * u + h)
                            last = pe.matmul(bank[VO][HD * h:HD * h + HD, 0:T],
                                             v_sb[0:SP_, c % 2, j, col:col + HD],
                                             probT[0:SP_, ST * h + j, :],
                                             start=(j == 0), stop=(j == ST - 1))
                    last.then_inc(pv_mm, 1)

            pe.wait_ge(ident_done, 1)
            pe.wait_ge(q_out, GROUPS)
            slots(pe, slot)


def kernel(x, ctx_2048, mask_BxS2_bf1, L0_xattn_Wq, L0_xattn_Wk, L0_xattn_Wv, L0_xattn_Wo,
           L0_xattn_ln_gamma, L0_xattn_ln_beta, L0_xattn_gate):
    import numpy as np
    import concourse.bacc as bacc
    from concourse.bass_utils import run_bass_kernel_spmd

    x = np.ascontiguousarray(x)
    arrays = {
        "in_xT": np.ascontiguousarray(x.reshape(B * T, D).T),
        "in_x": x,
        "in_ctx": np.ascontiguousarray(ctx_2048),
        "in_mask": np.ascontiguousarray(mask_BxS2_bf1).view(np.uint8),
        "in_wqT": np.ascontiguousarray(np.asarray(L0_xattn_Wq).T),
        "in_wkT": np.ascontiguousarray(np.asarray(L0_xattn_Wk).T),
        "in_wvT": np.ascontiguousarray(np.asarray(L0_xattn_Wv).T),
        "in_woT": np.ascontiguousarray(np.asarray(L0_xattn_Wo).T),
        "in_gamma": np.ascontiguousarray(np.asarray(L0_xattn_ln_gamma).reshape(KT, 128).T),
        "in_beta": np.ascontiguousarray(np.asarray(L0_xattn_ln_beta).reshape(KT, 128).T),
        "in_gate": np.ascontiguousarray(L0_xattn_gate),
    }
    nc = bacc.Bacc("TRN2", target_bir_lowering=False, num_devices=1)
    args = [nc.dram_tensor(n, a.shape, mybir.dt.from_np(a.dtype), kind="ExternalInput").ap()
            for n, a in arrays.items()]
    out = nc.dram_tensor("out", (B, T, D), F32, kind="ExternalOutput").ap()
    xattn(nc, *args, out)
    return run_bass_kernel_spmd(nc, [arrays], core_ids=[0]).results[0]["out"]
```

```python
from contextlib import ExitStack

import concourse.bass as bass
from concourse import mybir

F32 = mybir.dt.float32
F32R = mybir.dt.float32r
U8 = mybir.dt.uint8
ALU = mybir.AluOpType
ACT = mybir.ActivationFunctionType

B, T, S, D = 32, 112, 375, 512
HEADS, HD = 16, 32
KT = D // 128
HC = 128 // HD
ST, SP_ = 3, 125
SE = S + 1
GB = 4
GROUPS = B // GB
GN = GB * T
SLOTS = B * KT
LOOP = 2 * KT
SCALE = float(HD) ** -0.5
EPS = 1e-5
HIGHEST = 3.4e38
WARM_UP = 7
PASSES = ((0, 0), (0, 1), (1, 0))


def xattn(nc, xT, x, ctx, ctxT, mask, wqT, wkT, wvT, woT, gamma, beta, gate, out, row_stats):
    es = ExitStack()
    with es:
        def sb(name, shape, dt=F32):
            return es.enter_context(nc.sbuf_tensor(name, shape, dt))

        def sem(name):
            return es.enter_context(nc.semaphore(name))

        w_kvo = [sb(f"w_{w}", [128, 2, KT, D], F32R) for w in "kvo"]
        wk, wv, wo = w_kvo
        qT = sb("qT", [128, B, KT, T])
        flat = qT[:, :, :, :].rearrange("p b c t -> p (b c t)")
        WN = KT * D
        raw0 = B * KT * T - 4 * WN
        raw_k, raw_v, raw_o, raw_q = [
            flat[:, raw0 + i * WN:raw0 + (i + 1) * WN].rearrange("p (c n) -> p c n", c=KT)
            for i in (1, 2, 3, 0)]
        RAW_GROUP = raw0 // (KT * GN)

        shared_r = sb("shared_r", [128, 2 * WN + 4 * KT * GN], F32R)

        def cut_r(at, *shape):
            n = 1
            for k in shape:
                n *= k
            names = "abcd"[:len(shape)]
            ap = shared_r[:, at:at + n].rearrange(
                f"p ({' '.join(names)}) -> p {' '.join(names)}", **dict(zip(names, shape)))
            return at + n, ap

        at, xr = cut_r(0, 2, 2, KT, GN)
        at, wq = cut_r(at, 2, KT, D)
        at, cT = cut_r(0, 2, 2, KT, SE)
        at, kT = cut_r(at, 2, 2, SE)
        at, qr = cut_r(at, 2, 2, KT, T)
        at, oT = cut_r(at, 2, 2, KT, T)

        shared_f = sb("shared_f", [128, 2 * ST * D + 2 * HC * S + HC * ST * T])
        xraw = shared_f[:, 0:2 * KT * GN].rearrange("p (g c n) -> p g c n", g=2, c=KT)
        v_sb = shared_f[:, 0:2 * ST * D].rearrange("p (b j n) -> p b j n", b=2, j=ST)
        at = 2 * ST * D
        prob = shared_f[:, at:at + 2 * HC * S].rearrange("p (q h s) -> p q h s", q=2, h=HC)
        at += 2 * HC * S
        probT = shared_f[:, at:at + HC * ST * T].rearrange("p (i t) -> p i t", t=T)

        rows = sb("rows", [128, ST, D])
        cn = sb("cn", [128, 2, KT, S])
        stat_bc = sb("stat_bc", [128, 2, S])
        xy = sb("xy", [128, 2, D])
        mask_u8 = sb("mask_u8", [128, 2, S], U8)
        mask_b = sb("mask_b", [128, 2, S])
        ident = sb("ident", [128, 128])
        gam = sb("gam", [128, KT])
        bet = sb("bet", [128, KT])
        gat = sb("gat", [128, 1])
        stats = sb("stats", [128, ST, 6])
        mv = sb("mv", [128, 2, ST, 2])
        half = sb("half", [128, ST])
        vare = sb("vare", [128, ST])
        rs0 = sb("rs0", [128, ST])
        tmp = sb("tmp", [128, ST])
        row_stat = sb("row_stat", [128, 2, ST])
        ntop = sb("ntop", [128, 2, HC])
        den = sb("den", [128, 2, HC])
        rden = sb("rden", [128, 2, HC])

        bank = [es.enter_context(nc.psum_tensor(f"bank{i}", [128, 512], F32)) for i in range(8)]
        KB, VO, PA, PX = 4, 5, 6, 7

        ld_const = sem("ld_const")
        ld_w = {w: sem(f"ld_w{w}") for w in "kvo"}
        ld_wq = [sem(f"ld_wq{k}") for k in range(KT)]
        ld_x0 = [sem(f"ld_x0{k}") for k in range(KT)]
        ld_xT = [sem(f"ld_xT{i}") for i in range(2)]
        ld_rows = sem("ld_rows")
        stat_stored = sem("stat_stored")
        ld_stat = sem("ld_stat")
        ld_ctx = [sem(f"ld_ctx{i}") for i in range(2)]
        ld_x = [sem(f"ld_x{i}") for i in range(2)]
        ld_mask = [sem(f"ld_mask{i}") for i in range(2)]
        stored = [sem(f"stored{i}") for i in range(2)]
        ident_done = sem("ident_done")
        ident_step = sem("ident_step")
        pad_done = sem("pad_done")
        wq_hi = sem("wq_hi")
        wq_done = sem("wq_done")
        x0_hi = sem("x0_hi")
        x0_done = sem("x0_done")
        xr_hi = sem("xr_hi")
        xr_done = sem("xr_done")
        w_hi = sem("w_hi")
        w_done = sem("w_done")
        q_mm = sem("q_mm")
        q_out = sem("q_out")
        gate_done = sem("gate_done")
        bn_step = sem("bn_step")
        stats_done = sem("stats_done")
        ln_step = sem("ln_step")
        row_stat_done = sem("row_stat_done")
        ln_part = sem("ln_part")
        ln_done = sem("ln_done")
        qr_step = sem("qr_step")
        qr_done = sem("qr_done")
        mask_step = sem("mask_step")
        mask_done = sem("mask_done")
        c_hi = sem("c_hi")
        c_done = sem("c_done")
        k_mm = sem("k_mm")
        k_hi = sem("k_hi")
        k_done = sem("k_done")
        v_mm = sem("v_mm")
        v_done = sem("v_done")
        s_mm = sem("s_mm")
        max_done = sem("max_done")
        exp_done = sem("exp_done")
        rden_done = sem("rden_done")
        prob_done = sem("prob_done")
        t_mm = [sem(f"t_mm{i}") for i in range(3)]
        t_done = [sem(f"t_done{i}") for i in range(3)]
        pv_mm = sem("pv_mm")
        o_hi = sem("o_hi")
        o_done = sem("o_done")
        y_mm = sem("y_mm")
        y_done = sem("y_done")
        passed = sem("passed")

        block = es.enter_context(nc.Block())

        xT_v = xT.rearrange("(c p) n -> p c n", p=128)
        rows_v = ctx.rearrange("b (p j) d -> b p j d", j=ST)
        ctxT_v = ctxT.rearrange("b (c p) s -> b p c s", p=128)
        row_stats_v = row_stats.rearrange("b (w p j) -> b p w j", w=2, j=ST)
        wqT_v = wqT.rearrange("(c p) n -> p c n", p=128)
        wT = {"k": wkT, "v": wvT, "o": woT}

        def live(i, k, shift, count):
            return not isinstance(i, int) or 0 <= k * i + shift < count

        def first_two(i, c):
            return isinstance(i, int) and 2 * i + c < 2

        def wait_apart(engine, s, value):
            engine.wait_ge(s, value)
            if not isinstance(value, int):
                engine.sem_inc(passed)

        def slots(engine, slot, first=-1, last=SLOTS // LOOP + 1):
            for i in range(first, 1):
                for r in range(LOOP):
                    slot(i, r)
            with engine.Fori(1, SLOTS // LOOP - 2) as i:
                for r in range(LOOP):
                    slot(i, r)
            for i in range(SLOTS // LOOP - 2, last):
                for r in range(LOOP):
                    slot(i, r)

        def early(i, r):
            return isinstance(i, int) and 0 <= LOOP * i + r + 6 < KT

        def o_slot(i, r):
            if isinstance(i, int) and i == SLOTS // LOOP - 1 and r >= KT:
                return r == LOOP - 1
            return r % KT == 1 and live(i, 2, r // KT - 1, B)

        def ending(i, r):
            return isinstance(i, int) and LOOP * i + r >= SLOTS - 1

        def o_bank(i, r):
            return KB if ending(i, r) else VO

        def v_item(r):
            b, u = r // KT, r % KT
            return {2: (b + 1, 0), 3: (b + 1, 1), 0: (b, 2), 1: (b, None)}[u]

        @block.sync
        def _(sync):
            def load_xT(i, g):
                sync.dma_start(xraw[:, g, :, :], xT_v[:, :, bass.ds(i * (2 * GN) + g * GN, GN)]) \
                    .then_inc(ld_xT[g], 16)

            def load_w(w, dst):
                sync.dma_start(dst, wT[w].rearrange("(c p) n -> p c n", p=128)).then_inc(ld_w[w], 16)

            def load_ctx(i, c):
                sync.dma_start(cn[:, c % 2, :, :], ctxT_v[i * 2 + c, :, :, :]) \
                    .then_inc(ld_ctx[c % 2], 16)

            def load_rows(i, c):
                if not isinstance(i, int) or 2 * i + c > 0:
                    wait_apart(sync, stats_done, i * 2 + c)
                sync.dma_start(rows[0:SP_, :, :], rows_v[i * 2 + c, :, :, :]).then_inc(ld_rows, 16)

            def spread_stats(i, c):
                wait_apart(sync, row_stat_done, i * 2 + (c + 1))
                sync.dma_start(row_stats_v[i * 2 + c, :, :, :], row_stat[0:SP_, :, :]) \
                    .then_inc(stat_stored, 16)
                wait_apart(sync, stat_stored, i * 32 + (c + 1) * 16)
                if not isinstance(i, int) or 2 * i + c > 0:
                    wait_apart(sync, ln_done, i * 2 + c)
                sync.dma_start(stat_bc[:, :, :].rearrange("p w s -> p (w s)"),
                               row_stats[bass.ds(i * 2 + c, 1), :].partition_broadcast(128)
                               .rearrange("p a s -> p (a s)")).then_inc(ld_stat, 16)

            def load_mask(i, c):
                sync.dma_start(mask_u8[0:T, c % 2, :],
                               mask[bass.ds(i * 2 + c, 1), :].partition_broadcast(T)
                               .rearrange("p a s -> p (a s)")) \
                    .then_inc(ld_mask[c % 2], 16)

            def load_x(i, c):
                sync.dma_start(xy[0:T, c % 2, :], x[i * 2 + c, :, :]).then_inc(ld_x[c % 2], 16)

            for k in range(KT):
                sync.dma_start(raw_q[:, k, :], wqT_v[:, k, :]).then_inc(ld_wq[k], 16)
            sync.dma_start(gam[:, :], gamma).then_inc(ld_const, 16)
            sync.dma_start(bet[:, :], beta).then_inc(ld_const, 16)
            sync.dma_start(gat[:, :], gate.partition_broadcast(128)).then_inc(ld_const, 16)
            load_xT(0, 1)
            load_rows(0, 0)
            load_w("k", raw_k)
            sync.wait_ge(xr_done, 1)
            load_xT(1, 0)
            load_w("v", raw_v)
            sync.wait_ge(xr_done, 2)
            load_xT(1, 1)
            load_w("o", raw_o)
            load_ctx(0, 0)
            load_rows(0, 1)
            spread_stats(0, 0)
            with sync.Fori(2, GROUPS // 2) as i:
                for g in range(2):
                    wait_apart(sync, xr_done, i * 2 + (g - 1))
                    load_xT(i, g)
            load_ctx(0, 1)
            load_rows(0, 2)
            spread_stats(0, 1)
            for b in (0, 1):
                load_mask(0, b)
                load_x(0, b)
            spread_stats(0, 2)
            load_rows(0, 3)

            def slot(i, r):
                c, u = divmod(r, KT)
                started = not isinstance(i, int) or 2 * i + c >= 0
                if u == 1 and started and live(i, 2, c + 4, B):
                    load_rows(i, c + 4)
                if u == 2 and live(i, 2, c + 3, B) and not first_two(i, c + 3):
                    wait_apart(sync, c_done, i * LOOP + (c + 2) * KT)
                    load_ctx(i, c + 3)
                if u == 3 and started and live(i, 2, c + 3, B):
                    spread_stats(i, c + 3)
                if u:
                    return
                if live(i, 2, c - 1, B):
                    wait_apart(sync, y_done, i * 2 + c)
                    sync.dma_start(out[i * 2 + (c - 1), :, :], xy[0:T, (c + 1) % 2, :]) \
                        .then_inc(stored[(c + 1) % 2], 16)
                    if live(i, 2, c + 1, B):
                        wait_apart(sync, stored[(c + 1) % 2], (i + c) * 16)
                        load_x(i, c + 1)
                if live(i, 2, c + 2, B) and not first_two(i, c + 2):
                    wait_apart(sync, mask_done, i * 2 + (c + 1))
                    load_mask(i, c + 2)

            slots(sync, slot)
            sync.wait_ge(stored[0], 16 * (B // 2))
            sync.wait_ge(stored[1], 16 * (B // 2))

        @block.gpsimd
        def _(pool):
            pool.memset(ident[:, :], 0.0).then_inc(ident_step, 1)
            pool.memset(half[:, :], -0.5).then_inc(ident_step, 1)
            pool.wait_ge(ident_step, 2)
            pool.affine_select(out=ident[:, :], in_=ident[:, :], compare_op=ALU.not_equal, fill=1.0,
                               base=0, pattern=[[-1, 128]], channel_multiplier=1) \
                .then_inc(ident_done, 1)

            def split_q(i, c):
                src = qT[:, bass.ds(i * 2 + c, 1), :, :].rearrange("p a c t -> p (a c) t")
                if not first_two(i, c):
                    wait_apart(pool, s_mm, i * LOOP + (c - 1) * KT)
                pool.tensor_copy(qr[:, c % 2, 0, :, :], src).then_inc(qr_step, 1)
                wait_apart(pool, qr_step, i * 2 + (c + 1))
                pool.tensor_tensor(qr[:, c % 2, 1, :, :], src, qr[:, c % 2, 0, :, :].bitcast(F32),
                                   ALU.subtract).then_inc(qr_done, 1)

            def convert_mask(i, c):
                m = mask_b[0:T, c % 2, :]
                wait_apart(pool, ld_mask[c % 2], (i + c // 2 + 1) * 16)
                if not first_two(i, c):
                    wait_apart(pool, max_done, i * (LOOP * HC) + (c - 1) * KT * HC)
                pool.tensor_scalar(m, mask_u8[0:T, c % 2, :], -1.0, 3e38, ALU.add, ALU.mult) \
                    .then_inc(mask_step, 1)
                wait_apart(pool, mask_step, i * 2 + (c + 1))
                pool.tensor_scalar(m, m, 3e38, None, ALU.mult).then_inc(mask_done, 1)

            STEPS = 7
            steps = [0]

            def then(ins):
                ins.then_inc(ln_step, 1)
                steps[0] = steps[0] + 1
                wait_apart(pool, ln_step, steps[0])

            def row_statistics(i, c):
                P = SP_
                steps[0] = i * (2 * STEPS) + c * STEPS
                wait_apart(pool, stats_done, i * 2 + (c + 1))
                if not isinstance(i, int) or 2 * i + c > 0:
                    wait_apart(pool, stat_stored, i * 32 + c * 16)
                then(pool.tensor_scalar(row_stat[:P, 0, :], mv[:P, c % 2, :, 0], -1.0, None,
                                        ALU.mult))
                then(pool.tensor_scalar(vare[:P, :], mv[:P, c % 2, :, 1], EPS, None, ALU.add))
                then(pool.tensor_tensor(rs0[:P, :], vare[:P, :], half[:P, :], ALU.pow))
                then(pool.tensor_tensor(tmp[:P, :], vare[:P, :], rs0[:P, :], ALU.mult))
                then(pool.tensor_tensor(tmp[:P, :], tmp[:P, :], rs0[:P, :], ALU.mult))
                then(pool.tensor_scalar(tmp[:P, :], tmp[:P, :], -0.5, 1.5, ALU.mult, ALU.add))
                then(pool.tensor_tensor(row_stat[:P, 1, :], tmp[:P, :], rs0[:P, :], ALU.mult))
                pool.sem_inc(row_stat_done, 1)

            def normalise(i, c):
                wait_apart(pool, ld_stat, i * 32 + (c + 1) * 16)
                wait_apart(pool, ld_ctx[c % 2], (i + c // 2 + 1) * 16)
                chunks = [cn[:, c % 2, k, :] for k in range(KT)]
                for w, op in enumerate((ALU.add, ALU.mult)):
                    for chunk in chunks:
                        last = pool.tensor_tensor(chunk, chunk, stat_bc[:, w, :], op)
                    last.then_inc(ln_part, 1)
                    wait_apart(pool, ln_part, i * 4 + (2 * c + w + 1))
                for k, chunk in enumerate(chunks):
                    last = pool.tensor_scalar(chunk, chunk, gam[:, k:k + 1], bet[:, k:k + 1],
                                              ALU.mult, ALU.add)
                last.then_inc(ln_done, 1)

            def slot(i, r):
                if r % KT:
                    return
                c = r // KT
                if isinstance(i, int) and i == r == 0:
                    pool.wait_ge(q_out, GROUPS * KT)
                if live(i, 2, c + 2, B) and not first_two(i, c + 2):
                    normalise(i, c + 2)
                if live(i, 2, c + 1, B):
                    split_q(i, c + 1)
                    convert_mask(i, c + 1)
                if live(i, 2, c + 3, B) and (not isinstance(i, int) or 2 * i + c >= 0):
                    row_statistics(i, c + 3)

            row_statistics(0, 0)
            row_statistics(0, 1)
            pool.wait_ge(ld_const, 48)
            normalise(0, 0)
            normalise(0, 1)
            row_statistics(0, 2)
            for p in range(2):
                pool.wait_ge(q_mm, (GROUPS - 1 + p) * KT)
                pool.memset(cT[:, p, :, :, S:SE].rearrange("p b c s -> p (b c) s").bitcast(F32), 0.0) \
                    .then_inc(pad_done, 1)
            pool.wait_ge(q_out, KT)
            slots(pool, slot)

        @block.scalar
        def _(act):
            def load_x0(k):
                act.dma_start(xraw[:, 0, k, :], xT_v[:, k, 0:GN]).then_inc(ld_x0[k], 16)

            load_x0(0)
            act.wait_ge(ident_step, 2)
            act.activation(tmp[:, :], half[:, :], ACT.Copy)
            for k in range(1, KT):
                load_x0(k)
            for k in range(KT):
                act.wait_ge(ld_wq[k], 16)
                act.activation(wq[:, 0, k, :], raw_q[:, k, :], ACT.Copy).then_inc(wq_hi, 1)
            act.wait_ge(ld_const, 48)
            act.activation(gat[:, :], gat[:, :], ACT.Tanh).then_inc(gate_done, 1)

            def q_group(i, g):
                for m in range(KT):
                    act.wait_ge(q_mm, i * (2 * KT) + (g * KT + m + 1))
                    dst = qT[:, bass.ds(i * (2 * GB) + g * GB, GB), m, :]
                    act.activation(dst, bank[KT * g + m][:, 0:GN]
                                   .rearrange("p (b t) -> p b t", t=T), ACT.Copy).then_inc(q_out, 1)

            def context_hi(i, r):
                if not live(i, LOOP, r + 6, SLOTS):
                    return
                c, k = divmod(r + 6, KT)
                if k == 0:
                    act.wait_ge(ln_done, i * 2 + (c + 1))
                    if not first_two(i, c):
                        act.wait_ge(k_mm, i * LOOP + (c - 1) * KT)
                        act.wait_ge(v_mm, i * (2 * ST) + (c - 1) * ST)
                act.activation(cT[:, c % 2, 0, k, 0:S], cn[:, c % 2, k, :], ACT.Copy) \
                    .then_inc(c_hi, 1)

            def weight_hi(w, raw, dst):
                act.wait_ge(ld_w[w], 16)
                for k in range(KT):
                    act.activation(dst[:, 0, k, :], raw[:, k, :], ACT.Copy).then_inc(w_hi, 1)

            weight_hi("k", raw_k, wk)
            q_group(0, 0)
            weight_hi("v", raw_v, wv)
            weight_hi("o", raw_o, wo)
            q_group(0, 1)
            act.wait_ge(wq_done, KT)
            act.wait_ge(w_done, 3 * KT)
            with act.Fori(1, GROUPS // 2 - 1) as i:
                for g in range(2):
                    q_group(i, g)
            q_group(GROUPS // 2 - 1, 0)
            for r in range(LOOP - 6, LOOP - 6 + KT):
                context_hi(-1, r)
            q_group(GROUPS // 2 - 1, 1)

            def slot(i, r):
                if live(i, LOOP, r - 2, SLOTS):
                    p, u = (r - 2) // KT % 2, (r - 2) % KT
                    act.wait_ge(pv_mm, i * LOOP + (r - 1))
                    act.activation(oT[:, p, 0, u, :], bank[VO][:, 0:T], ACT.Copy).then_inc(o_hi, 1)
                transposed(i, r, 0)
                c, j = v_item(r)
                v_live = j is not None and live(i, 2, c, B)
                group_2_early = not (v_live or o_slot(i, r))
                if group_2_early:
                    transposed(i, r, 2)
                if live(i, LOOP, r, SLOTS):
                    for h in range(HC):
                        act.wait_ge(max_done, i * (LOOP * HC) + (r * HC + h + 1))
                        last = act.activation(prob[0:T, r % 2, h, :], prob[0:T, r % 2, h, :], ACT.Exp,
                                              bias=ntop[0:T, r % 2, h:h + 1], scale=-1.0,
                                              accum_out=den[0:T, r % 2, h:h + 1])
                    last.then_inc(exp_done, 1)
                if v_live:
                    act.wait_ge(v_mm, i * (2 * ST) + (c * ST + j + 1))
                    act.activation(v_sb[0:SP_, c % 2, j, :], bank[VO][0:SP_, :], ACT.Copy) \
                        .then_inc(v_done, 1)
                if not group_2_early:
                    transposed(i, r, 2)
                if not early(i, r):
                    context_hi(i, r)
                if live(i, LOOP, r + 2, SLOTS):
                    act.wait_ge(k_mm, i * LOOP + (r + 3))
                    act.activation(kT[:, r % 2, 0, :], bank[KB][:, 0:SE], ACT.Copy).then_inc(k_hi, 1)

            def transposed(i, r, g):
                if live(i, LOOP, r - 1, SLOTS):
                    act.wait_ge(t_mm[g], i * LOOP + r)
                    if not isinstance(i, int) or LOOP * i + r - 1 > 0:
                        act.wait_ge(pv_mm, i * LOOP + (r - 1))
                    act.activation(probT[0:SP_, HC * g:HC * g + HC, :].rearrange("p i t -> p (i t)"),
                                   bank[PA][0:SP_, 0:HC * T], ACT.Copy).then_inc(t_done[g], 1)

            slots(act, slot)

        @block.vector
        def _(dve):
            def split(src, hi, lo, s_hi, count, s_done):
                dve.tensor_copy(hi, src).then_inc(s_hi, 1)
                dve.wait_ge(s_hi, count)
                dve.tensor_tensor(lo, src, hi.bitcast(F32), ALU.subtract).then_inc(s_done, 1)

            for k in range(KT):
                dve.wait_ge(ld_x0[k], 16)
                dve.tensor_copy(xr[:, 0, 0, k, :], xraw[:, 0, k, :]).then_inc(x0_hi, 1)
                dve.wait_ge(wq_hi, k + 1)
                dve.tensor_tensor(wq[:, 1, k, :], raw_q[:, k, :], wq[:, 0, k, :].bitcast(F32),
                                  ALU.subtract).then_inc(wq_done, 1)
                dve.wait_ge(x0_hi, k + 1)
                dve.tensor_tensor(xr[:, 0, 1, k, :], xraw[:, 0, k, :],
                                  xr[:, 0, 0, k, :].bitcast(F32), ALU.subtract) \
                    .then_inc(x0_done if k < KT - 1 else xr_done, 1)

            def x_group(i, g):
                dve.wait_ge(ld_xT[g], (i + g) * 16)
                if not isinstance(i, int) or i > 0:
                    dve.wait_ge(q_mm, i * (2 * KT) + (g - 1) * KT)
                split(xraw[:, g, :, :], xr[:, g, 0, :, :], xr[:, g, 1, :, :],
                      xr_hi, i * 2 + g, xr_done)

            def statistics(i, c):
                dve.wait_ge(ld_rows, i * 32 + (c + 1) * 16)
                if not first_two(i, c):
                    dve.wait_ge(row_stat_done, i * 2 + (c - 1))
                if isinstance(i, int) and 0 < 2 * i + c < 3:
                    dve.wait_ge(stats_done, 2 * i + c)
                for j in range(ST):
                    dve.bn_stats(stats[0:SP_, j, :], rows[0:SP_, j, :]).then_inc(bn_step, 1)
                wait_apart(dve, bn_step, i * (2 * ST) + (c + 1) * ST)
                for j in range(ST):
                    last = dve.bn_aggr(mv[0:SP_, c % 2, j, :], stats[0:SP_, j, :])
                last.then_inc(stats_done, 1)

            def weight_lo(n, raw, dst):
                for k in range(KT):
                    dve.wait_ge(w_hi, n * KT + k + 1)
                    dve.tensor_tensor(dst[:, 1, k, :], raw[:, k, :], dst[:, 0, k, :].bitcast(F32),
                                      ALU.subtract).then_inc(w_done, 1)

            x_group(0, 1)
            statistics(0, 0)
            weight_lo(0, raw_k, wk)
            x_group(1, 0)
            weight_lo(1, raw_v, wv)
            x_group(1, 1)
            weight_lo(2, raw_o, wo)
            statistics(0, 1)
            with dve.Fori(2, GROUPS // 2) as i:
                for g in range(2):
                    x_group(i, g)
            statistics(0, 2)

            def context_lo(i, r):
                if not live(i, LOOP, r + 6, SLOTS):
                    return
                p, k = (r + 6) // KT % 2, (r + 6) % KT
                dve.wait_ge(c_hi, i * LOOP + (r + 7))
                dve.tensor_tensor(cT[:, p, 1, k, 0:S], cn[:, p, k, :],
                                  cT[:, p, 0, k, 0:S].bitcast(F32), ALU.subtract) \
                    .then_inc(c_done, 1)

            def result(i, r):
                c = r // KT - 1
                if r < KT:
                    dve.wait_ge(ld_x[1], i * 16)
                else:
                    dve.wait_ge(ld_x[0], (i + 1) * 16)
                dve.wait_ge(gate_done, 1)
                dve.wait_ge(y_mm, i * 2 + (c + 1))
                dve.scalar_tensor_tensor(xy[0:T, c % 2, :], bank[o_bank(i, r)][0:T, :],
                                         gat[0:T, 0:1],
                                         xy[0:T, c % 2, :], ALU.mult, ALU.add) \
                    .then_inc(y_done, 1)

            def transposed_1(i, r):
                if live(i, LOOP, r - 1, SLOTS):
                    dve.wait_ge(t_mm[1], i * LOOP + r)
                    if not isinstance(i, int) or LOOP * i + r - 1 > 0:
                        dve.wait_ge(pv_mm, i * LOOP + (r - 1))
                    dve.tensor_copy(probT[0:SP_, HC:2 * HC, :].rearrange("p i t -> p (i t)"),
                                    bank[PX][0:SP_, 0:HC * T]).then_inc(t_done[1], 1)

            for r in range(LOOP - 6, LOOP - 6 + KT):
                context_lo(-1, r)

            def slot(i, r):
                if live(i, LOOP, r - 2, SLOTS):
                    p, u = (r - 2) // KT % 2, (r - 2) % KT
                    dve.wait_ge(o_hi, i * LOOP + (r - 1))
                    dve.tensor_tensor(oT[:, p, 1, u, :], bank[VO][:, 0:T],
                                      oT[:, p, 0, u, :].bitcast(F32), ALU.subtract) \
                        .then_inc(o_done, 1)
                if live(i, LOOP, r, SLOTS):
                    q, c = r % 2, r // KT
                    if r % KT == 0:
                        dve.wait_ge(mask_done, i * 2 + (c + 1))
                    wait_apart(dve, s_mm, i * LOOP + (r + 1))
                    if not isinstance(i, int) or LOOP * i + r >= 2:
                        wait_apart(dve, t_mm[2], i * LOOP + (r - 1))
                    for h in range(HC):
                        dve.tensor_tensor_reduce(
                            out=prob[0:T, q, h, :], in0=bank[h][0:T, 0:S], in1=mask_b[0:T, c, :],
                            scale=-SCALE, scalar=HIGHEST, op0=ALU.add, op1=ALU.min,
                            accum_out=ntop[0:T, q, h:h + 1]).then_inc(max_done, 1)
                        if h == 1:
                            transposed_1(i, r)
                else:
                    transposed_1(i, r)
                if r % KT == 0 and live(i, LOOP, r, SLOTS) and live(i, 2, r // KT + 3, B):
                    statistics(i, r // KT + 3)
                if o_slot(i, r) and not ending(i, r):
                    result(i, r)
                if live(i, LOOP, r, SLOTS):
                    q = r % 2
                    dve.wait_ge(exp_done, i * LOOP + (r + 1))
                    dve.reciprocal(rden[0:T, q, :], den[0:T, q, :]).then_inc(rden_done, 1)
                    dve.wait_ge(rden_done, i * LOOP + (r + 1))
                    for h in range(HC):
                        last = dve.tensor_scalar(prob[0:T, q, h, :], prob[0:T, q, h, :],
                                                 rden[0:T, q, h:h + 1], None, ALU.mult)
                    last.then_inc(prob_done, 1)
                if o_slot(i, r) and ending(i, r):
                    result(i, r)
                if not early(i, r):
                    context_lo(i, r)
                if live(i, LOOP, r + 2, SLOTS):
                    dve.wait_ge(k_hi, i * LOOP + (r + 3))
                    dve.tensor_tensor(kT[:, r % 2, 1, :], bank[KB][:, 0:SE],
                                      kT[:, r % 2, 0, :].bitcast(F32), ALU.subtract) \
                        .then_inc(k_done, 1)

            slots(dve, slot)

        @block.tensor
        def _(pe):
            def product(dst, pairs, start=True, stop=True):
                for k, (l, m) in enumerate(pairs):
                    last = pe.matmul(dst, l, m, start=(start and k == 0),
                                     stop=(stop and k == len(pairs) - 1))
                return last

            def output(i, r, c, chunks):
                return product(bank[o_bank(i, r)][0:T, :],
                               [(oT[:, c % 2, a, k, :], wo[:, d, k, :])
                                for k in chunks for a, d in PASSES],
                               start=(chunks[0] == 0), stop=(chunks[-1] == KT - 1))

            def q_group(i, g):
                pe.wait_ge(xr_done, i * 2 + (g + 1))
                if not isinstance(i, int) or i > 0:
                    pe.wait_ge(q_out, i * (2 * KT) + (g - 1) * KT)
                for k in range(KT):
                    for m in range(KT):
                        for e, (a, c) in enumerate(PASSES):
                            last = q_pass(g, k, m, a, c, e)
                        if k == KT - 1:
                            last.then_inc(q_mm, 1)

            def q_pass(g, k, m, a, c, e):
                return pe.matmul(bank[KT * g + m][:, 0:GN],
                                 wq[:, a, k, 128 * m:128 * m + 128], xr[:, g, c, k, :],
                                 start=(k == 0 and e == 0),
                                 stop=(k == KT - 1 and e == len(PASSES) - 1))

            def first_q_group():
                for k in range(KT):
                    for e, (a, c) in enumerate(((0, 0), (1, 0), (0, 1))):
                        if e == 0:
                            pe.wait_ge(x0_hi, k + 1)
                            pe.wait_ge(wq_hi, k + 1)
                        elif e == 1:
                            pe.wait_ge(wq_done, k + 1)
                        elif k < KT - 1:
                            pe.wait_ge(x0_done, k + 1)
                        else:
                            pe.wait_ge(xr_done, 1)
                        for m in range(KT):
                            last = q_pass(0, k, m, a, c, e)
                            if k == KT - 1 and e == len(PASSES) - 1:
                                last.then_inc(q_mm, 1)

            pe.wait_ge(ident_done, 1)
            for _ in range(WARM_UP):
                pe.matmul(bank[7][:, 0:128], ident[:, :], ident[:, :], start=True, stop=True)
            first_q_group()
            q_group(0, 1)
            with pe.Fori(1, GROUPS // 2) as i:
                for g in range(2):
                    q_group(i, g)

            def transpose_probs(i, r, g):
                for e in range(HC):
                    h, j = divmod(HC * g + e, ST)
                    last = pe.transpose(bank[PX if g == 1 else PA][0:SP_, e * T:(e + 1) * T],
                                        prob[0:T, (r - 1) % 2, h, SP_ * j:SP_ * j + SP_],
                                        ident[0:T, 0:T])
                last.then_inc(t_mm[g], 1)

            def group_2(i, r):
                pe.wait_ge(t_done[0], i * LOOP + r)
                transpose_probs(i, r, 2)

            def slot(i, r):
                here = live(i, LOOP, r, SLOTS)
                before = live(i, LOOP, r - 1, SLOTS)
                if here:
                    c, u, q = r // KT, r % KT, r % 2
                    if u == 0:
                        pe.wait_ge(qr_done, i * 2 + (c + 1))
                    pe.wait_ge(k_done, i * LOOP + (r + 1))
                    if not isinstance(i, int) or LOOP * i + r > 0:
                        pe.wait_ge(max_done, i * (LOOP * HC) + r * HC)
                    for k, (a, d) in enumerate(PASSES):
                        for h in range(HC):
                            rows = slice(HD * h, HD * h + HD)
                            last = pe.matmul(bank[h][0:T, 0:SE], qr[rows, c, a, u, :], kT[rows, q, d, :],
                                             start=(k == 0), stop=(k == len(PASSES) - 1))
                    last.then_inc(s_mm, 1)
                if before:
                    if isinstance(i, int) and LOOP * i + r == 1:
                        pe.wait_ge(q_out, GROUPS * KT)
                    pe.wait_ge(prob_done, i * LOOP + r)
                    if not isinstance(i, int) or LOOP * i + r - 1 > 0:
                        pe.wait_ge(t_done[2], i * LOOP + (r - 1))
                        pe.wait_ge(t_done[1], i * LOOP + (r - 1))
                    transpose_probs(i, r, 0)
                    transpose_probs(i, r, 1)
                c, j = v_item(r)
                v_live = j is not None and live(i, 2, c, B)
                if v_live:
                    pe.wait_ge(c_done, i * LOOP + (c + 1) * KT)
                    if live(i, LOOP, r - 2, SLOTS):
                        pe.wait_ge(o_done, i * LOOP + (r - 1))
                    elif 2 * i + c > 0 or j > 0:
                        pe.wait_ge(v_done, i * (2 * ST) + (c * ST + j))
                    product(bank[VO][0:SP_, :],
                            [(cT[:, c % 2, d, k, SP_ * j:SP_ * j + SP_], wv[:, a, k, :])
                             for k in range(KT) for a, d in PASSES]).then_inc(v_mm, 1)
                o_live = o_slot(i, r)
                if before and ending(i, r):
                    group_2(i, r)
                if o_live and not ending(i, r):
                    pe.wait_ge(o_done, i * LOOP + (r - 1))
                    output(i, r, r // KT - 1, range(KT)).then_inc(y_mm, 1)
                if isinstance(i, int) and LOOP * i + r == SLOTS - 1:
                    pe.wait_ge(o_done, (B - 1) * KT)
                    pe.wait_ge(k_done, SLOTS)
                    output(i, r, B - 2, range(KT)).then_inc(y_mm, 1)
                if isinstance(i, int) and LOOP * i + r == SLOTS:
                    pe.wait_ge(o_done, SLOTS - 1)
                    pe.wait_ge(y_done, B - 1)
                    output(i, r, B - 1, range(KT - 1))
                if isinstance(i, int) and LOOP * i + r == SLOTS + 1:
                    pe.wait_ge(o_done, SLOTS)
                    output(i, r, B - 1, range(KT - 1, KT)).then_inc(y_mm, 1)
                if before and not ending(i, r):
                    group_2(i, r)
                if live(i, LOOP, r + 2, SLOTS):
                    c, u = (r + 2) // KT, (r + 2) % KT
                    if u == 0:
                        pe.wait_ge(c_done, i * LOOP + (c + 1) * KT)
                        pe.wait_ge(pad_done, 1 if first_two(i, c) and c % 2 == 0 else 2)
                        pe.wait_ge(w_done, 3 * KT)
                    if not isinstance(i, int) or LOOP * i + r + 2 > 0:
                        pe.wait_ge(k_done, i * LOOP + (r + 2))
                    product(bank[KB][:, 0:SE],
                            [(wk[:, a, k, 128 * u:128 * u + 128], cT[:, c % 2, d, k, :])
                             for k in range(KT) for a, d in PASSES]).then_inc(k_mm, 1)
                if before:
                    c, u = (r - 1) // KT, (r - 1) % KT
                    for g in range(3):
                        pe.wait_ge(t_done[g], i * LOOP + r)
                    if u == 0:
                        pe.wait_ge(v_done, i * (2 * ST) + (c + 1) * ST)
                    vc, vj = v_item(r)
                    if v_live:
                        pe.wait_ge(v_done, i * (2 * ST) + (vc * ST + vj + 1))
                    elif o_live and not ending(i, r):
                        pe.wait_ge(y_done, i * 2 + r // KT)
                    elif live(i, LOOP, r - 2, SLOTS):
                        pe.wait_ge(o_done, i * LOOP + (r - 1))
                    for j in range(ST):
                        for h in range(HC):
                            col = HD * (HC * u + h)
                            last = pe.matmul(bank[VO][HD * h:HD * h + HD, 0:T],
                                             v_sb[0:SP_, c % 2, j, col:col + HD],
                                             probT[0:SP_, ST * h + j, :],
                                             start=(j == 0), stop=(j == ST - 1))
                    last.then_inc(pv_mm, 1)

            pe.wait_ge(q_out, (GROUPS - 1) * KT + VO - KT + 1)
            slots(pe, slot)


def kernel(x, ctx_2048, mask_BxS2_bf1, L0_xattn_Wq, L0_xattn_Wk, L0_xattn_Wv, L0_xattn_Wo,
           L0_xattn_ln_gamma, L0_xattn_ln_beta, L0_xattn_gate):
    import numpy as np
    import concourse.bacc as bacc
    from concourse.bass_utils import run_bass_kernel_spmd

    x = np.ascontiguousarray(x)
    arrays = {
        "in_xT": np.ascontiguousarray(x.reshape(B * T, D).T),
        "in_x": x,
        "in_ctx": np.ascontiguousarray(ctx_2048),
        "in_ctxT": np.ascontiguousarray(np.asarray(ctx_2048).transpose(0, 2, 1)),
        "in_mask": np.ascontiguousarray(mask_BxS2_bf1).view(np.uint8),
        "in_wqT": np.ascontiguousarray(np.asarray(L0_xattn_Wq).T),
        "in_wkT": np.ascontiguousarray(np.asarray(L0_xattn_Wk).T),
        "in_wvT": np.ascontiguousarray(np.asarray(L0_xattn_Wv).T),
        "in_woT": np.ascontiguousarray(np.asarray(L0_xattn_Wo).T),
        "in_gamma": np.ascontiguousarray(np.asarray(L0_xattn_ln_gamma).reshape(KT, 128).T),
        "in_beta": np.ascontiguousarray(np.asarray(L0_xattn_ln_beta).reshape(KT, 128).T),
        "in_gate": np.ascontiguousarray(L0_xattn_gate),
    }
    nc = bacc.Bacc("TRN2", target_bir_lowering=False, num_devices=1)
    args = [nc.dram_tensor(n, a.shape, mybir.dt.from_np(a.dtype), kind="ExternalInput").ap()
            for n, a in arrays.items()]
    out = nc.dram_tensor("out", (B, T, D), F32, kind="ExternalOutput").ap()
    row_stats = nc.dram_tensor("row_stats", (B, 2 * S), F32, kind="Internal").ap()
    xattn(nc, *args, out, row_stats)
    return run_bass_kernel_spmd(nc, [arrays], core_ids=[0]).results[0]["out"]
```
